# Optimizing a Trainium2 kernel written in Bass

```python
import numpy as np
import jax
import jax.numpy as jnp

def _softmax(x, axis=-1):
    return jax.nn.softmax(x, axis=axis)

def _gelu(x):
    return jax.nn.gelu(x, approximate=True)

def _silu(x):
    return jax.nn.silu(x)

def _sigmoid(x):
    return jax.nn.sigmoid(x)

def _layernorm(x, axis=-1, eps=1e-05):
    m = jnp.mean(x, axis=axis, keepdims=True)
    v = jnp.var(x, axis=axis, keepdims=True)
    return (x - m) / jnp.sqrt(v + eps)

def _scatter_add(tgt, idx, src, axis=0):
    return tgt.at[idx].add(src)

def _segment_sum(src, seg, n):
    return jax.ops.segment_sum(src, seg, n)
kernel_name = 'mk_vit_tower_d1_tok_img768_r4_26435b'

def setup_inputs(seed: int=0):
    np.random.seed(seed)
    _w = jnp.asarray

    def _rec_inputs():
        import jax
        import jax.numpy as jnp
        _rk = jax.random.key(seed)
        x = -0.000356955 + 1 * jax.random.normal(jax.random.fold_in(_rk, 1), (16, 3, 96, 96), jnp.float32)
        return x
    x = _rec_inputs()

    def _L0_tok_setup():
        import jax, jax.numpy as jnp
        import numpy as np
        PATCH = 16
        POS_GRID = (14, 14)
        EMBED = 192
        C_IN = 3

        def _nearest_resize(x, out_h, out_w):
            _, _, h, w = x.shape
            ih = jnp.arange(out_h) * h // out_h
            iw = jnp.arange(out_w) * w // out_w
            return x[:, :, ih][:, :, :, iw]
        key = jax.random.key(seed)
        k1, k2, k3, k4, k5 = jax.random.split(key, 5)
        im = jax.random.normal(k1, (128, C_IN, 224, 224), dtype=jnp.float32)
        W = jax.random.normal(k2, (C_IN * PATCH * PATCH, EMBED), dtype=jnp.float32) * 0.02
        b = jax.random.normal(k3, (EMBED,), dtype=jnp.float32) * 0.02
        positions = jax.random.normal(k4, (1, EMBED, POS_GRID[0], POS_GRID[1]), dtype=jnp.float32)
        cls_embedding = jax.random.normal(k5, (1, 1, EMBED), dtype=jnp.float32)
        return {'im': im, 'W': W, 'b': b, 'positions': positions, 'cls_embedding': cls_embedding}
    _L0_tok_all = _L0_tok_setup()
    _L0_tok_in = {k: v for k, v in _L0_tok_all.items() if k in ('W', 'b', 'positions', 'cls_embedding')}
    del _L0_tok_all

    def _L0_attn_setup():
        import jax, jax.numpy as jnp
        import numpy as np
        DIM = 192
        HEADS = 12
        HEAD_DIM = DIM // HEADS
        EPS = 1e-12

        def _l1_normalize(t):
            denom = jnp.maximum(jnp.sum(jnp.abs(t), axis=-2, keepdims=True), EPS)
            return t / denom
        key = jax.random.key(seed)
        k1, k2, k3 = jax.random.split(key, 3)
        x = jax.random.normal(k1, (8, 1024, DIM), dtype=jnp.float32)
        s = 1.0 / np.sqrt(DIM)
        w_qkv = jax.random.uniform(k2, (3 * DIM, DIM), dtype=jnp.float32, minval=-s, maxval=s)
        w_proj = jax.random.uniform(k3, (DIM, DIM), dtype=jnp.float32, minval=-s, maxval=s)
        b_proj = jnp.zeros((DIM,), dtype=jnp.float32)
        return {'x': x, 'w_qkv': w_qkv, 'w_proj': w_proj, 'b_proj': b_proj}
    _L0_attn_all = _L0_attn_setup()
    _L0_attn_in = {k: v for k, v in _L0_attn_all.items() if k in ('w_qkv', 'w_proj', 'b_proj')}
    del _L0_attn_all

    def _L0_ffn_setup():
        import jax, jax.numpy as jnp
        import numpy as np
        H = 192
        I = 96
        E = 16
        G = 4
        TOPK_GROUP = 2
        TOP_K = 4
        SCALE = 2.5
        N_SHARED = 2
        IS = I * N_SHARED
        B, S = (1, 512)

        def _route(x, router_w, router_b, corr_bias):
            logits = x.astype(jnp.float32) @ router_w.T + router_b
            scores = jax.nn.sigmoid(logits)
            sfc = scores + corr_bias[None, :]
            grp = sfc.reshape(-1, G, E // G)
            group_scores = jax.lax.top_k(grp, 2)[0].sum(-1)
            _, gidx = jax.lax.top_k(group_scores, TOPK_GROUP)
            gmask = jax.nn.one_hot(gidx, G, dtype=sfc.dtype).sum(axis=1)
            score_mask = jnp.repeat(gmask, E // G, axis=-1)
            sfc = jnp.where(score_mask > 0, sfc, 0.0)
            _, idx = jax.lax.top_k(sfc, TOP_K)
            w = jnp.take_along_axis(scores, idx, axis=1)
            w = w / (w.sum(-1, keepdims=True) + 1e-20)
            return (idx, w * SCALE)

        def _forward(x3, router_w, router_b, corr_bias, gWg, gbg, gWu, gbu, gWd, gbd, sWg, sbg, sWu, sbu, sWd, sbd):
            orig_shape = x3.shape
            x = x3.reshape(-1, H)
            idx, w = _route(x, router_w, router_b, corr_bias)
            c = (jax.nn.one_hot(idx, E, dtype=w.dtype) * w[..., None]).sum(1)
            h = jax.nn.silu(jnp.einsum('th,ehi->tei', x, gWg) + gbg) * (jnp.einsum('th,ehi->tei', x, gWu) + gbu)
            out_e = jnp.einsum('tei,eih->teh', h, gWd) + gbd
            moe_out = jnp.einsum('te,teh->th', c, out_e)
            hs = jax.nn.silu(x @ sWg + sbg) * (x @ sWu + sbu)
            shared = hs @ sWd + sbd
            return (moe_out + shared).reshape(orig_shape)
        key = jax.random.key(seed)
        ks = jax.random.split(key, 16)
        s = lambda k, shape, fan: jax.random.normal(k, shape, jnp.float32) * fan ** (-0.5)
        return {'hidden_states': jax.random.normal(ks[0], (B, S, H), jnp.float32), 'router_w': s(ks[1], (E, H), H), 'router_b': jnp.zeros((E,), jnp.float32), 'corr_bias': jnp.zeros((E,), jnp.float32), 'gWg': s(ks[2], (E, H, I), H), 'gbg': jnp.zeros((E, I), jnp.float32), 'gWu': s(ks[3], (E, H, I), H), 'gbu': jnp.zeros((E, I), jnp.float32), 'gWd': s(ks[4], (E, I, H), I), 'gbd': jnp.zeros((E, H), jnp.float32), 'sWg': s(ks[5], (H, IS), H), 'sbg': jnp.zeros((IS,), jnp.float32), 'sWu': s(ks[6], (H, IS), H), 'sbu': jnp.zeros((IS,), jnp.float32), 'sWd': s(ks[7], (IS, H), IS), 'sbd': jnp.zeros((H,), jnp.float32)}
    _L0_ffn_all = _L0_ffn_setup()
    _L0_ffn_in = {k: v for k, v in _L0_ffn_all.items() if k in ('router_w', 'router_b', 'corr_bias', 'gWg', 'gbg', 'gWu', 'gbu', 'gWd', 'gbd', 'sWg', 'sbg', 'sWu', 'sbu', 'sWd', 'sbd')}
    del _L0_ffn_all
    return {'x': x, 'L0_tok_W': _L0_tok_in['W'], 'L0_tok_b': _L0_tok_in['b'], 'L0_tok_positions': _L0_tok_in['positions'], 'L0_tok_cls_embedding': _L0_tok_in['cls_embedding'], 'L0_attn_w_qkv': _L0_attn_in['w_qkv'], 'L0_attn_w_proj': _L0_attn_in['w_proj'], 'L0_attn_b_proj': _L0_attn_in['b_proj'], 'L0_ffn_router_w': _L0_ffn_in['router_w'], 'L0_ffn_router_b': _L0_ffn_in['router_b'], 'L0_ffn_corr_bias': _L0_ffn_in['corr_bias'], 'L0_ffn_gWg': _L0_ffn_in['gWg'], 'L0_ffn_gbg': _L0_ffn_in['gbg'], 'L0_ffn_gWu': _L0_ffn_in['gWu'], 'L0_ffn_gbu': _L0_ffn_in['gbu'], 'L0_ffn_gWd': _L0_ffn_in['gWd'], 'L0_ffn_gbd': _L0_ffn_in['gbd'], 'L0_ffn_sWg': _L0_ffn_in['sWg'], 'L0_ffn_sbg': _L0_ffn_in['sbg'], 'L0_ffn_sWu': _L0_ffn_in['sWu'], 'L0_ffn_sbu': _L0_ffn_in['sbu'], 'L0_ffn_sWd': _L0_ffn_in['sWd'], 'L0_ffn_sbd': _L0_ffn_in['sbd']}

def reference(x, L0_tok_W, L0_tok_b, L0_tok_positions, L0_tok_cls_embedding, L0_attn_w_qkv, L0_attn_w_proj, L0_attn_b_proj, L0_ffn_router_w, L0_ffn_router_b, L0_ffn_corr_bias, L0_ffn_gWg, L0_ffn_gbg, L0_ffn_gWu, L0_ffn_gbu, L0_ffn_gWd, L0_ffn_gbd, L0_ffn_sWg, L0_ffn_sbg, L0_ffn_sWu, L0_ffn_sbu, L0_ffn_sWd, L0_ffn_sbd):
    import jax
    import jax.numpy as jnp

    def _L0_tok_ref(im, W, b, positions, cls_embedding):
        import jax, jax.numpy as jnp
        import numpy as np
        PATCH = 16
        POS_GRID = (14, 14)
        EMBED = 192
        C_IN = 3

        def _nearest_resize(x, out_h, out_w):
            _, _, h, w = x.shape
            ih = jnp.arange(out_h) * h // out_h
            iw = jnp.arange(out_w) * w // out_w
            return x[:, :, ih][:, :, :, iw]
        B, C, H, Wd = im.shape
        ph, pw = (PATCH, PATCH)
        gh, gw = (H // ph, Wd // pw)
        patches = im.reshape(B, C, gh, ph, gw, pw)
        patches = patches.transpose(0, 2, 4, 1, 3, 5).reshape(B, gh * gw, C * ph * pw)
        pos = _nearest_resize(positions, gh, gw)
        pos = pos.reshape(1, EMBED, gh * gw).transpose(0, 2, 1)
        embeds = jnp.einsum('bsp,pd->bsd', patches, W) + b + pos
        cls_tok = jnp.broadcast_to(cls_embedding, (B, 1, EMBED))
        return jnp.concatenate((cls_tok, embeds), axis=1)

    def _L0_attn_ref(x, w_qkv, w_proj, b_proj):
        import jax, jax.numpy as jnp
        import numpy as np
        DIM = 192
        HEADS = 12
        HEAD_DIM = DIM // HEADS
        EPS = 1e-12

        def _l1_normalize(t):
            denom = jnp.maximum(jnp.sum(jnp.abs(t), axis=-2, keepdims=True), EPS)
            return t / denom
        B, N, C = x.shape
        hd = C // HEADS
        qkv = x @ w_qkv.T
        qkv = qkv.reshape(B, N, 3, HEADS, hd).transpose(2, 0, 3, 1, 4)
        q, k, v = (qkv[0], qkv[1], qkv[2])
        q = _l1_normalize(q)
        k = _l1_normalize(k)
        if N < hd:
            out = jnp.einsum('bhnd,bhmd,bhme->bhne', q, k, v)
        else:
            kv = jnp.einsum('bhnd,bhne->bhde', k, v)
            out = jnp.einsum('bhnd,bhde->bhne', q, kv)
        out = out.transpose(0, 2, 1, 3).reshape(B, N, C)
        return out @ w_proj.T + b_proj

    def _L0_ffn_ref(hidden_states, router_w, router_b, corr_bias, gWg, gbg, gWu, gbu, gWd, gbd, sWg, sbg, sWu, sbu, sWd, sbd):
        import jax, jax.numpy as jnp
        import numpy as np
        H = 192
        I = 96
        E = 16
        G = 4
        TOPK_GROUP = 2
        TOP_K = 4
        SCALE = 2.5
        N_SHARED = 2
        IS = I * N_SHARED
        B, S = (1, 512)

        def _route(x, router_w, router_b, corr_bias):
            logits = x.astype(jnp.float32) @ router_w.T + router_b
            scores = jax.nn.sigmoid(logits)
            sfc = scores + corr_bias[None, :]
            grp = sfc.reshape(-1, G, E // G)
            group_scores = jax.lax.top_k(grp, 2)[0].sum(-1)
            _, gidx = jax.lax.top_k(group_scores, TOPK_GROUP)
            gmask = jax.nn.one_hot(gidx, G, dtype=sfc.dtype).sum(axis=1)
            score_mask = jnp.repeat(gmask, E // G, axis=-1)
            sfc = jnp.where(score_mask > 0, sfc, 0.0)
            _, idx = jax.lax.top_k(sfc, TOP_K)
            w = jnp.take_along_axis(scores, idx, axis=1)
            w = w / (w.sum(-1, keepdims=True) + 1e-20)
            return (idx, w * SCALE)

        def _forward(x3, router_w, router_b, corr_bias, gWg, gbg, gWu, gbu, gWd, gbd, sWg, sbg, sWu, sbu, sWd, sbd):
            orig_shape = x3.shape
            x = x3.reshape(-1, H)
            idx, w = _route(x, router_w, router_b, corr_bias)
            c = (jax.nn.one_hot(idx, E, dtype=w.dtype) * w[..., None]).sum(1)
            h = jax.nn.silu(jnp.einsum('th,ehi->tei', x, gWg) + gbg) * (jnp.einsum('th,ehi->tei', x, gWu) + gbu)
            out_e = jnp.einsum('tei,eih->teh', h, gWd) + gbd
            moe_out = jnp.einsum('te,teh->th', c, out_e)
            hs = jax.nn.silu(x @ sWg + sbg) * (x @ sWu + sbu)
            shared = hs @ sWd + sbd
            return (moe_out + shared).reshape(orig_shape)
        return _forward(hidden_states, router_w, router_b, corr_bias, gWg, gbg, gWu, gbu, gWd, gbd, sWg, sbg, sWu, sbu, sWd, sbd)
    h = _L0_tok_ref(x, L0_tok_W, L0_tok_b, L0_tok_positions, L0_tok_cls_embedding)
    h = h + _L0_attn_ref(_layernorm(h, axis=-1), L0_attn_w_qkv, L0_attn_w_proj, L0_attn_b_proj)
    h = h + _L0_ffn_ref(_layernorm(h, axis=-1), L0_ffn_router_w, L0_ffn_router_b, L0_ffn_corr_bias, L0_ffn_gWg, L0_ffn_gbg, L0_ffn_gWu, L0_ffn_gbu, L0_ffn_gWd, L0_ffn_gbd, L0_ffn_sWg, L0_ffn_sbg, L0_ffn_sWu, L0_ffn_sbu, L0_ffn_sWd, L0_ffn_sbd)
    return h

_drawn_inputs = setup_inputs


def setup_inputs(seed=0):
    import zlib

    import numpy as np

    out = dict(_drawn_inputs(seed))
    spreads = {'L0_attn_b_proj': (0.0, 0.1),
     'L0_ffn_router_b': (0.0, 0.1),
     'L0_ffn_corr_bias': (0.0, 0.1),
     'L0_ffn_gbg': (0.0, 0.1),
     'L0_ffn_gbu': (0.0, 0.1),
     'L0_ffn_gbd': (0.0, 0.1),
     'L0_ffn_sbg': (0.0, 0.1),
     'L0_ffn_sbu': (0.0, 0.1),
     'L0_ffn_sbd': (0.0, 0.1)}
    factors = {}
    for name, (base, spread) in spreads.items():
        noise = np.random.default_rng([zlib.crc32(name.encode()), seed]).standard_normal(out[name].shape)
        drawn = base * np.exp(spread * noise) if base else spread * noise
        out[name] = jnp.asarray(drawn.astype(out[name].dtype))
    for name, factor in factors.items():
        out[name] = (out[name] * factor).astype(out[name].dtype)
    return out
```

```python
import numpy as np
import concourse.bass as bass
from concourse import mybir
from contextlib import ExitStack

IMAGES, CHANNELS, SIDE, PATCH = 16, 3, 96, 16
GRID = SIDE // PATCH
POS_SIDE = 14
D = 192
TOK = GRID * GRID + 1
T = IMAGES * TOK
TILES = [(t, min(128, T - t)) for t in range(0, T, 128)]
NT = len(TILES)
PATCH_K = CHANNELS * PATCH * PATCH // 128
HEAD, HALF_D = 16, D // 2
SLOT = 64
EVEN = TOK + 1
HALF_T = T // 2
HALF_I = IMAGES // 2
PAIRS = IMAGES // 2
EXPERTS, GROUPS, INNER = 16, 4, 96
PER_GROUP = EXPERTS // GROUPS
TOP_GROUPS, TOP_K, SCALE = 2, 4, 2.5
ROUTED, SHARED = EXPERTS * INNER, 2 * INNER
HID = ROUTED + SHARED
BLOCKS = [(a, min(128, SHARED - a)) for a in range(0, SHARED, 128)]
SHARED_MB = len(BLOCKS)
BLOCKS += [(a, 128) for a in range(SHARED, HID, 128)]
MB = len(BLOCKS)
UNITS = [(m, j) for m in range(MB) for j in range(2)]
NU = len(UNITS)
LN_EPS, L1_EPS, SUM_EPS = 1e-5, 1e-12, 1e-20
XW = 3 * D + EXPERTS
CROWS = 2 * EXPERTS + 1
PAD, TAKEN = -3e38, 3e38


def rows_of(m):
    return BLOCKS[m][1]


_at = 0
COLS = {}
for _name, _n in (("ident", 128), ("token_is_patch", NT), ("b", D), ("base", NT * D), ("patch_w", PATCH_K * D),
                  ("blocks", D), ("b_proj", D), ("w_proj", 2 * D), ("router_b", EXPERTS), ("corr", EXPERTS),
                  ("before", GROUPS * GROUPS), ("after", GROUPS * GROUPS), ("gate_b", MB), ("up_b", MB)):
    COLS[_name] = (_at, _at + _n)
    _at += _n
FIRST_COLS = COLS["blocks"][0]
SMALL_COLS = _at

CHUNK = 2
CHUNKS = MB // CHUNK
RAW_SLOTS = 3
LAG = 3
DOWN_LAG = LAG + 3
ROUTE_AT = 2 * SHARED_MB + LAG
MOE_SLOTS = 10
T_SLOTS, S_SLOTS, H_SLOTS, BLOCK_SLOTS = ROUTE_AT + 1, 3, 3, 3


def tower(nc, patches, small, x_w, moe_w, down_w, down_b, spread, out):
    dt = mybir.dt
    f32, f32r = dt.float32, dt.float32r
    ALU = mybir.AluOpType
    ACT = mybir.ActivationFunctionType
    AX = mybir.AxisListType

    with ExitStack() as ctx:
        def sb(name, shape, t=f32):
            return ctx.enter_context(nc.sbuf_tensor(name, shape, t))

        def sem(name):
            return ctx.enter_context(nc.semaphore(name))

        patch_sb = sb("patch_sb", [128, PATCH_K * T])
        small_sb = sb("small_sb", [128, SMALL_COLS])
        xw_raw = sb("xw_raw", [128, 2, XW])
        moe_raw = sb("moe_raw", [128, RAW_SLOTS, CHUNK * 512])
        down_raw = patch_sb[:, 0:MB * D].rearrange("p (m d) -> p m d", d=D)
        down_b_raw = sb("down_b_raw", [CROWS, D])
        spread_raw = sb("spread_raw", [CROWS, ROUTED])
        xw_hi = sb("xw_hi", [128, 2, XW], f32r)
        xw_lo = sb("xw_lo", [128, 2, XW], f32r)
        moe_hi = sb("moe_hi", [128, MOE_SLOTS, 512], f32r)
        moe_lo = sb("moe_lo", [128, MOE_SLOTS, 512], f32r)
        down_hi = sb("down_hi", [128, MB, D], f32r)
        down_lo = sb("down_lo", [128, MB, D], f32r)
        down_b_hi = sb("down_b_hi", [CROWS, D], f32r)
        down_b_lo = sb("down_b_lo", [CROWS, D], f32r)
        spread_sb = sb("spread_sb", [CROWS, ROUTED], f32r)
        h_tok = sb("h_tok", [128, NT, D])
        h2_tok = sb("h2_tok", [128, NT, D])
        stats = sb("stats", [128, 2, 6])
        mean_var = sb("mean_var", [128, 2 * NT, 2])
        root = sb("root", [128, 2 * NT, 4])
        normed = sb("normed", [128, 2, D])
        split_tok = sb("split_tok", [128, 2, 2 * D], f32r)
        out_tok = sb("out_tok", [128, 2, D])
        x1T = sb("x1T", [128, 3, IMAGES, SLOT], f32r)
        x2T = x1T[:, :, :, :].rearrange("p i m t -> p i (m t)")[:, :, 0:T]
        sums = sb("sums", [HALF_D, 2, 2, 2, HALF_I])
        scale_qk = sb("scale_qk", [HALF_D, 2, 2, HALF_I])
        qT = sb("qT", [HALF_D, 2, T])
        kv_tok = sb("kv_tok", [128, 2, 2 * D])
        shared_buf = sb("shared_buf", [128, max(IMAGES * D, T_SLOTS * HALF_T)])
        kv_blocks = shared_buf[0:HALF_D, 0:IMAGES * D].rearrange("p (i d) -> p i d", d=D)
        attnT = sb("attnT", [HALF_D, 2, T])
        logits = sb("logits", [128, NT, EXPERTS])
        scores = sb("scores", [128, NT, EXPERTS])
        choice = sb("choice", [128, NT, EXPERTS])
        pair_sums = sb("pair_sums", [128, NT * GROUPS, 6])
        group_s = sb("group_s", [128, NT, GROUPS])
        beaten = sb("beaten", [128, 2, NT, GROUPS * GROUPS])
        rank = sb("rank", [128, NT, GROUPS])
        masked = sb("masked", [128, NT, EXPERTS + TOP_K])
        top8 = sb("top8", [128, NT, 8])
        taken8 = sb("taken8", [128, NT, 8])
        marked = sb("marked", [128, NT, EXPERTS + TOP_K])
        weight = sb("weight", [128, NT, EXPERTS])
        w_sum = sb("w_sum", [128, 3, NT])
        combine = sb("combine", [128, NT, EXPERTS])
        combine_split = sb("combine_split", [128, NT, CROWS], f32r)
        combineT = sb("combineT", [CROWS, T], f32r)
        silu_g = sb("silu_g", [128, S_SLOTS, HALF_T])
        prod = shared_buf[:, 0:T_SLOTS * HALF_T].rearrange("p (s t) -> p s t", t=HALF_T)
        hid = sb("hid", [128, H_SLOTS, HALF_T])
        hid_hi = sb("hid_hi", [128, BLOCK_SLOTS, T], f32r)
        hid_lo = sb("hid_lo", [128, BLOCK_SLOTS, T], f32r)

        ps = ctx.enter_context(nc.psum_tensor("ps", [128, 8, 512], f32))

        def col(name):
            a, b = COLS[name]
            return small_sb[:, a:b]

        ident = col("ident")
        base = col("base").rearrange("p (t d) -> p t d", d=D)
        patch_w = col("patch_w").rearrange("p (k d) -> p k d", d=D)
        w_proj = col("w_proj").rearrange("p (m d) -> p m d", d=D)
        split_f = split_tok[:, :, :].bitcast(f32)
        combine_split_f = combine_split[:, :, :].bitcast(f32)

        s_patch = [sem(f"s_patch{t}") for t in range(NT)]
        s_first, s_small, s_xw, s_consts = sem("s_first"), sem("s_small"), sem("s_xw"), sem("s_consts")
        s_moe_in = [sem(f"s_moe_in{i}") for i in range(RAW_SLOTS)]
        s_down_in = sem("s_down_in")
        s_moe_hi, s_moe_lo = sem("s_moe_hi"), sem("s_moe_lo")
        s_xw_hi, s_xw_lo = sem("s_xw_hi"), sem("s_xw_lo")
        s_down_hi, s_down_lo = sem("s_down_hi"), sem("s_down_lo")
        s_spread = sem("s_spread")
        s_zero = sem("s_zero")
        s_base = sem("s_base")
        s_embed = sem("s_embed")
        s_var = sem("s_var")
        s_root = sem("s_root")
        s_normed = sem("s_normed")
        s_tok_hi, s_tok_lo = sem("s_tok_hi"), sem("s_tok_lo")
        s_turned = sem("s_turned")
        s_xT = sem("s_xT")
        s_k, s_q = sem("s_k"), sem("s_q")
        s_k_used, s_q_used = sem("s_k_used"), sem("s_q_used")
        s_kv, s_kv_tok = sem("s_kv"), sem("s_kv_tok")
        s_outer, s_blocks = sem("s_outer"), sem("s_blocks")
        s_attn, s_attnT = sem("s_attn"), sem("s_attnT")
        s_hb = sem("s_hb")
        s_h = sem("s_h")
        s_proj = sem("s_proj")
        s_h2 = sem("s_h2")
        s_logits_ps, s_logits, s_scores = sem("s_logits_ps"), sem("s_logits"), sem("s_scores")
        s_combine, s_combine_ps, s_combineT = sem("s_combine"), sem("s_combine_ps"), sem("s_combineT")
        s_gate, s_up, s_spread_ps = sem("s_gate"), sem("s_up"), sem("s_spread_ps")
        s_silu, s_prod, s_hid = sem("s_silu"), sem("s_prod"), sem("s_hid")
        s_hid_hi, s_hid_lo = sem("s_hid_hi"), sem("s_hid_lo")
        s_block_down = sem("s_block_down")
        s_down, s_out_tok = sem("s_down"), sem("s_out_tok")
        s_stored = [sem(f"s_stored{i}") for i in range(2)]
        s_dve, s_pool = sem("s_dve"), sem("s_pool")

        block = ctx.enter_context(nc.Block())

        @block.sync
        def _(sp):
            def load_patches(t):
                a, n = TILES[t]
                sp.dma_start(patch_sb[:, PATCH_K * a:PATCH_K * (a + n)],
                             patches[:, PATCH_K * a:PATCH_K * (a + n)]).then_inc(s_patch[t], 16)

            sp.dma_start(small_sb[:, 0:FIRST_COLS], small[:, 0:FIRST_COLS]).then_inc(s_first, 16)
            for t in range(NT):
                load_patches(t)
                if t == 1:
                    sp.dma_start(xw_raw[:, :, :], x_w).then_inc(s_xw, 16)
            sp.dma_start(small_sb[:, FIRST_COLS:SMALL_COLS], small[:, FIRST_COLS:SMALL_COLS]).then_inc(s_small, 16)
            sp.dma_start(spread_raw[:, :], spread).then_inc(s_consts, 16)
            sp.dma_start(down_b_raw[:, :], down_b).then_inc(s_consts, 16)
            for c in range(CHUNKS):
                if c >= RAW_SLOTS:
                    sp.wait_ge(s_moe_hi, CHUNK * (c - RAW_SLOTS + 1))
                    sp.wait_ge(s_moe_lo, CHUNK * (c - RAW_SLOTS + 1))
                a = 512 * CHUNK * c
                sp.dma_start(moe_raw[:, c % RAW_SLOTS, :], moe_w[:, a:a + 512 * CHUNK]).then_inc(s_moe_in[c % RAW_SLOTS], 16)
                if c == 4:
                    sp.wait_ge(s_embed, NT)
                    sp.dma_start(down_raw, down_w).then_inc(s_down_in, 16)
            for t, (a, n) in enumerate(TILES):
                sp.wait_ge(s_out_tok, t + 1)
                sp.dma_start(out[a:a + n, :], out_tok[0:n, t % 2, :]).then_inc(s_stored[t % 2], 16)
            for i in range(2):
                sp.wait_ge(s_stored[i], 16 * len(range(i, NT, 2)))

        @block.tensor
        def _(pe):
            def product(o, hi, lo, wide, cols, narrow, tokens_are_weights=False):
                x = wide
                terms = ((hi[0], 0), (lo[0], 0), (hi[0], 2), (hi[1], 1), (lo[1], 1))
                for i, (w, part) in enumerate(terms):
                    w = w[:, cols[0]:cols[1]]
                    a, b = (x(part), w) if tokens_are_weights else (w, x(part))
                    last = pe.matmul(o, a, b, start=(i == 0), stop=(i == len(terms) - 1))
                return last

            def turn(t, count):
                a, n = TILES[t % NT]
                pe.wait_ge(s_tok_hi, t + 1)
                pe.wait_ge(s_tok_lo, t + 1)
                if t >= 2:
                    pe.wait_ge(s_xT, t - 1)
                if t == NT:
                    pe.wait_ge(s_blocks, PAIRS)
                for i in range(3):
                    last = pe.transpose(ps[:, 2 + t % 2, 128 * i:128 * i + n],
                                        split_f[0:n, t % 2, 128 * i:128 * i + 128], ident[0:n, 0:n])
                last.then_inc(s_turned, 1)

            pe.wait_ge(s_first, 16)
            for t, (a, n) in enumerate(TILES):
                pe.wait_ge(s_patch[t], 16)
                if t >= 2:
                    pe.wait_ge(s_h, t - 1)
                tile = patch_sb[:, PATCH_K * a:PATCH_K * (a + n)].rearrange("p (k t) -> p k t", k=PATCH_K)
                for k in range(PATCH_K):
                    last = pe.matmul(ps[0:n, t % 2, 0:D], tile[:, k, :], patch_w[:, k, :],
                                     start=(k == 0), stop=(k == PATCH_K - 1))
                last.then_inc(s_embed, 1)
                if t >= 2:
                    turn(t - 2, t - 1)
            turn(NT - 2, NT - 1)
            turn(NT - 1, NT)

            xh = [xw_hi[:, 0, :], xw_hi[:, 1, :]]
            xl = [xw_lo[:, 0, :], xw_lo[:, 1, :]]
            pe.wait_ge(s_xw_hi, 1)
            pe.wait_ge(s_xw_lo, 1)

            for u in range(4):
                j, m = u // 2, u % 2
                pe.wait_ge(s_xT, 3 if j == 0 else NT)
                pe.wait_ge(s_zero, 1)
                im = slice(HALF_I * j, HALF_I * (j + 1))
                for kind, sem_, used, bank in ((1, s_k, s_k_used, 4), (0, s_q, s_q_used, 6)):
                    if u >= 2:
                        pe.wait_ge(used, u - 1)
                    c = D * kind + HALF_D * m
                    product(ps[0:HALF_D, bank + u % 2, 0:HALF_I * EVEN], xh, xl, lambda i: x1T[:, i, im, 0:EVEN],
                            (c, c + HALF_D), None).then_inc(sem_, 1)

            def two_images(p, i):
                return x1T[:, i, 2 * p:2 * p + 2, :].rearrange("p m t -> p (m t)")

            def outer(p):
                pe.wait_ge(s_kv_tok, p + 1)
                if p >= 2:
                    pe.wait_ge(s_blocks, p - 1)
                if p == 1:
                    pe.wait_ge(s_k_used, 4)
                for m in range(2):
                    for i in range(2):
                        r = slice(64 * i, 64 * i + TOK)
                        last = pe.matmul(ps[0:HALF_D, 2 + 2 * (p % 2) + i, HALF_D * m:HALF_D * (m + 1)],
                                         kv_tok[r, p % 2, HALF_D * m:HALF_D * (m + 1)],
                                         kv_tok[r, p % 2, D + HALF_D * m:D + HALF_D * (m + 1)],
                                         start=True, stop=True)
                last.then_inc(s_outer, 1)

            for p in range(PAIRS):
                if p >= 2:
                    pe.wait_ge(s_kv_tok, p - 1)
                if p == 0:
                    pe.wait_ge(s_h, NT)
                product(ps[:, p % 2, 0:2 * D], xh, xl, lambda i: two_images(p, i), (D, 3 * D), None,
                        True).then_inc(s_kv, 1)
                if p >= 1:
                    outer(p - 1)
            outer(PAIRS - 1)

            for v in range(4):
                j, m = v // 2, v % 2
                pe.wait_ge(s_q_used, 4)
                pe.wait_ge(s_blocks, PAIRS if j else PAIRS // 2)
                if v >= 2:
                    pe.wait_ge(s_attnT, v - 1)
                for i in range(HALF_I):
                    im = HALF_I * j + i
                    last = pe.matmul(ps[0:HALF_D, 6 + m, TOK * i:TOK * (i + 1)],
                                     kv_blocks[:, im, HALF_D * m:HALF_D * (m + 1)],
                                     qT[:, m, TOK * im:TOK * (im + 1)], start=True, stop=True)
                last.then_inc(s_attn, 1)

            pe.wait_ge(s_small, 16)

            def route(t):
                a, n = TILES[t]
                pe.wait_ge(s_xT, NT + t + 1)
                product(ps[0:n, 4, EXPERTS * t:EXPERTS * (t + 1)], xh, xl, lambda i: x2T[:, i, a:a + n],
                        (3 * D, XW), None, True).then_inc(s_logits_ps, 1)

            for t, (a, n) in enumerate(TILES):
                pe.wait_ge(s_attnT, 2 if a + n <= HALF_T else 4)
                if t == 0:
                    pe.wait_ge(s_kv_tok, PAIRS)
                if t >= 2:
                    pe.wait_ge(s_h2, t - 1)
                for m in range(2):
                    last = pe.matmul(ps[0:n, t % 2, 0:D], attnT[:, m, a:a + n], w_proj[0:HALF_D, m, :],
                                     start=(m == 0), stop=(m == 1))
                last.then_inc(s_proj, 1)
                if t >= 2:
                    turn(NT + t - 2, 0)
            turn(2 * NT - 2, 0)
            turn(2 * NT - 1, 0)
            for t in range(NT):
                route(t)

            def gate_up(u):
                m, j = UNITS[u]
                r = rows_of(m)
                if j == 0:
                    pe.wait_ge(s_moe_hi, m + 1)
                    pe.wait_ge(s_moe_lo, m + 1)
                if u == 0:
                    pe.wait_ge(s_h2, NT)
                    pe.wait_ge(s_xT, 2 * NT)
                if u >= 2:
                    pe.wait_ge(s_silu, u - 1)
                tok = slice(HALF_T * j, HALF_T * (j + 1))
                hi, lo = moe_hi[:, m % MOE_SLOTS, :], moe_lo[:, m % MOE_SLOTS, :]
                for at, bank, done in ((0, 0, s_gate), (2 * r, 2, s_up)):
                    if bank == 2 and u >= 2:
                        pe.wait_ge(s_prod, u - 1)
                    product(ps[0:r, bank + u % 2, 0:HALF_T],
                            [hi[:, at:at + r], hi[:, at + r:at + 2 * r]], [lo[:, at:at + r], lo[:, at + r:at + 2 * r]],
                            lambda i: x2T[:, i, tok], (0, r), None).then_inc(done, 1)

            def spread_combine(u):
                m, j = UNITS[u]
                pe.wait_ge(s_hid, u)
                c = BLOCKS[m][0] - SHARED
                pe.matmul(ps[:, 7, 0:HALF_T], spread_sb[:, c:c + 128],
                          combineT[:, HALF_T * j:HALF_T * (j + 1)], start=True, stop=True).then_inc(s_spread_ps, 1)

            def turn_combine():
                pe.wait_ge(s_combine, 1)
                for t, (a, n) in enumerate(TILES):
                    bank, c = (7, 128 * t) if t < 4 else (6, 0)
                    last = pe.transpose(ps[0:CROWS, bank, c:c + n], combine_split_f[0:n, t, :], ident[0:n, 0:n])
                last.then_inc(s_combine_ps, 1)
                pe.wait_ge(s_combineT, 2)
                pe.wait_ge(s_spread, 1)

            def gather(t):
                return ps[0:TILES[t][1], 4 + t // 2, D * (t % 2):D * (t % 2 + 1)]

            def down_bias():
                pe.wait_ge(s_down_hi, 2)
                pe.wait_ge(s_down_lo, 2)
                for t, (a, n) in enumerate(TILES):
                    for i, w in enumerate((down_b_hi, down_b_lo)):
                        pe.matmul(gather(t), combineT[:, a:a + n], w[:, :], start=(i == 0 and t % 2 == 0), stop=False,
                                  skip_group_check=True)

            def down(m):
                r = rows_of(m)
                pe.wait_ge(s_hid_hi, 2 * m + 2)
                pe.wait_ge(s_hid_lo, 2 * m + 2)
                for t, (a, n) in enumerate(TILES):
                    for i, (x, w) in enumerate(((hid_hi, down_hi), (hid_hi, down_lo), (hid_lo, down_hi))):
                        last = pe.matmul(gather(t), x[0:r, m % BLOCK_SLOTS, a:a + n], w[0:r, m, :], start=False,
                                         stop=(m == MB - 1 and i == 2), skip_group_check=True)
                    if m == MB - 1:
                        last.then_inc(s_down, 1)
                if m < MB - 1:
                    last.then_inc(s_block_down, 1)

            for step in range(NU + DOWN_LAG):
                if step == ROUTE_AT:
                    turn_combine()
                    down_bias()
                if step < NU:
                    gate_up(step)
                if step >= ROUTE_AT and step - LAG < NU:
                    spread_combine(step - LAG)
                u = step - DOWN_LAG
                if u >= 0 and u % 2 == 1:
                    down(u // 2)

        @block.scalar
        def _(act):
            def root_of(t):
                n = TILES[t % NT][1]
                act.wait_ge(s_var, t + 1)
                act.activation(root[0:n, t, 1:2], root[0:n, t, 0:1], ACT.Sqrt).then_inc(s_root, 1)

            def high_of(t):
                n = TILES[t % NT][1]
                act.wait_ge(s_normed, t + 1)
                if t >= 2:
                    act.wait_ge(s_turned, t - 1)
                act.activation(split_tok[0:n, t % 2, 0:D], normed[0:n, t % 2, :], ACT.Copy).then_inc(s_tok_hi, 1)

            def take_xT(t):
                a, n = TILES[t % NT]
                act.wait_ge(s_turned, t + 1)
                turned = ps[:, 2 + t % 2, 0:384].rearrange("p (i t) -> p i t", i=3)
                if t >= NT:
                    last = act.activation(x2T[:, :, a:a + n], turned[:, :, 0:n], ACT.Copy)
                else:
                    first, end = -(-a // TOK), (a + n) // TOK
                    if a % TOK:
                        k = first * TOK - a
                        last = act.activation(x1T[:, :, first - 1, TOK - k:TOK], turned[:, :, 0:k], ACT.Copy)
                    k = first * TOK - a
                    w = (end - first) * TOK
                    for i in range(3):
                        last = act.activation(x1T[:, i, first:end, 0:TOK],
                                              turned[:, i, k:k + w].rearrange("p (m t) -> p m t", t=TOK), ACT.Copy)
                    if (a + n) % TOK:
                        last = act.activation(x1T[:, :, end, 0:(a + n) % TOK], turned[:, :, k + w:n], ACT.Copy)
                last.then_inc(s_xT, 1)

            def split_moe(m):
                c = m // CHUNK
                w = 4 * rows_of(m)
                act.wait_ge(s_moe_in[c % RAW_SLOTS], 16 * (c // RAW_SLOTS + 1))
                if m >= MOE_SLOTS:
                    act.wait_ge(s_up, 2 * (m - MOE_SLOTS + 1))
                act.activation(moe_hi[:, m % MOE_SLOTS, 0:w], moe_raw[:, c % RAW_SLOTS, 512 * (m % CHUNK):512 * (m % CHUNK) + w],
                               ACT.Copy).then_inc(s_moe_hi, 1)

            act.wait_ge(s_xw, 16)
            act.activation(xw_hi[:, :, :], xw_raw[:, :, :], ACT.Copy).then_inc(s_xw_hi, 1)
            for t in range(NT + 2):
                if t < NT:
                    root_of(t)
                if 1 <= t <= NT:
                    high_of(t - 1)
                if t >= 2:
                    take_xT(t - 2)
            done = 0
            for p in range(PAIRS):
                act.wait_ge(s_kv, p + 1)
                if p >= 2:
                    act.wait_ge(s_outer, p - 1)
                act.activation(kv_tok[:, p % 2, :], ps[:, p % 2, 0:2 * D], ACT.Copy).then_inc(s_kv_tok, 1)
                split_moe(p)
            for v in range(4):
                act.wait_ge(s_attn, v + 1)
                j, m = v // 2, v % 2
                act.activation(attnT[:, m, HALF_T * j:HALF_T * (j + 1)], ps[0:HALF_D, 6 + m, 0:HALF_T],
                               ACT.Copy).then_inc(s_attnT, 1)
            act.wait_ge(s_consts, 32)
            act.activation(spread_sb[:, :], spread_raw[:, :], ACT.Copy).then_inc(s_spread, 1)
            act.activation(down_b_hi[:, :], down_b_raw[:, :], ACT.Copy).then_inc(s_down_hi, 1)
            for t in range(NT + 2):
                if t < NT:
                    root_of(NT + t)
                if 1 <= t <= NT:
                    high_of(NT + t - 1)
                if t >= 2:
                    take_xT(NT + t - 2)
            act.wait_ge(s_logits, 1)
            act.activation(scores[:, :, :], logits[:, :, :], ACT.Sigmoid).then_inc(s_scores, 1)

            def high_hid(u):
                m, j = UNITS[u]
                r = rows_of(m)
                act.wait_ge(s_hid, u + 1)
                if m >= BLOCK_SLOTS:
                    act.wait_ge(s_block_down, m - BLOCK_SLOTS + 1)
                act.activation(hid_hi[0:r, m % BLOCK_SLOTS, HALF_T * j:HALF_T * (j + 1)], hid[0:r, u % H_SLOTS, :],
                               ACT.Copy).then_inc(s_hid_hi, 1)

            for u in range(NU + LAG + 1):
                if u < NU:
                    m, j = UNITS[u]
                    r = rows_of(m)
                    act.wait_ge(s_gate, u + 1)
                    if u >= S_SLOTS:
                        act.wait_ge(s_prod, u - S_SLOTS + 1)
                    act.activation(silu_g[0:r, u % S_SLOTS, :], ps[0:r, u % 2, 0:HALF_T], ACT.Silu,
                                   bias=col("gate_b")[0:r, m:m + 1]).then_inc(s_silu, 1)
                if u % 2 == 1 and u // 2 < MB - PAIRS:
                    split_moe(PAIRS + u // 2)
                if u == 0:
                    act.wait_ge(s_down_in, 16)
                    act.activation(down_hi[:, :, :], down_raw, ACT.Copy).then_inc(s_down_hi, 1)
                if u >= LAG + 1:
                    high_hid(u - LAG - 1)

        @block.gpsimd
        def _(pool):
            pool.memset(x1T[:, :, :, TOK:SLOT].bitcast(f32), 0.0)
            pool.memset(logits[:, :, :], 0.0)
            pool.memset(masked[:, :, :], PAD)
            pool.memset(taken8[:, :, :], PAD)
            pool.memset(combine_split[:, :, 2 * EXPERTS:CROWS].bitcast(f32), 1.0).then_inc(s_zero, 1)
            pool.wait_ge(s_xw_hi, 1)
            pool.tensor_tensor(xw_lo[:, :, :], xw_raw[:, :, :], xw_hi[:, :, :].bitcast(f32),
                               ALU.subtract).then_inc(s_xw_lo, 1)
            pool.wait_ge(s_small, 16)
            for t, (a, n) in enumerate(TILES):
                pool.wait_ge(s_h, t + 1)
                pool.tensor_tensor(h2_tok[0:n, t, :], h_tok[0:n, t, :], col("b_proj")[0:n, :], ALU.add).then_inc(s_hb, 1)
            def split_moe(m):
                c = m // CHUNK
                w = 4 * rows_of(m)
                pool.wait_ge(s_moe_hi, m + 1)
                pool.tensor_tensor(moe_lo[:, m % MOE_SLOTS, 0:w],
                                   moe_raw[:, c % RAW_SLOTS, 512 * (m % CHUNK):512 * (m % CHUNK) + w],
                                   moe_hi[:, m % MOE_SLOTS, 0:w].bitcast(f32), ALU.subtract).then_inc(s_moe_lo, 1)

            for m in range(PAIRS):
                split_moe(m)
            pool.wait_ge(s_down_hi, 2)
            pool.tensor_tensor(down_b_lo[:, :], down_b_raw[:, :], down_b_hi[:, :].bitcast(f32),
                               ALU.subtract).then_inc(s_down_lo, 1)
            pool.tensor_tensor(down_lo[:, :, :], down_raw, down_hi[:, :, :].bitcast(f32),
                               ALU.subtract).then_inc(s_down_lo, 1)
            for u in range(NU):
                m, j = UNITS[u]
                r = rows_of(m)
                if PAIRS + u < MB:
                    split_moe(PAIRS + u)
                tok = slice(HALF_T * j, HALF_T * (j + 1))
                pool.wait_ge(s_hid_hi, u + 1)
                pool.tensor_tensor(hid_lo[0:r, m % BLOCK_SLOTS, tok], hid[0:r, u % H_SLOTS, :],
                                   hid_hi[0:r, m % BLOCK_SLOTS, tok].bitcast(f32), ALU.subtract).then_inc(s_hid_lo, 1)

        @block.vector
        def _(dve):
            links = [0]

            def link(ins):
                links[0] += 1
                ins.then_inc(s_dve, 1)
                dve.wait_ge(s_dve, links[0])

            def moments(t, h):
                n = TILES[t % NT][1]
                link(dve.bn_stats(stats[0:n, t % 2, :], h[0:n, t % NT, :]))
                link(dve.bn_aggr(mean_var[0:n, t, :], stats[0:n, t % 2, :]))
                dve.tensor_scalar(root[0:n, t, 0:1], mean_var[0:n, t, 1:2], LN_EPS, None, ALU.add).then_inc(s_var, 1)

            def normalize(t, h):
                n = TILES[t % NT][1]
                v, r, g, y = root[0:n, t, 0:1], root[0:n, t, 1:2], root[0:n, t, 2:3], root[0:n, t, 3:4]
                dve.wait_ge(s_root, t + 1)
                link(dve.reciprocal(g, r))
                link(dve.scalar_tensor_tensor(out=y, in0=g, scalar=v, in1=g, op0=ALU.mult, op1=ALU.mult))
                link(dve.tensor_scalar(r, y, -0.5, 1.5, ALU.mult, ALU.add))
                link(dve.tensor_tensor(y, r, g, ALU.mult))
                if t >= 2:
                    dve.wait_ge(s_tok_hi, t - 1)
                dve.tensor_scalar(normed[0:n, t % 2, :], h[0:n, t % NT, :], mean_var[0:n, t, 0:1], y,
                                  ALU.subtract, ALU.mult).then_inc(s_normed, 1)

            def low_of(t):
                n = TILES[t % NT][1]
                dve.wait_ge(s_tok_hi, t + 1)
                dve.tensor_tensor(split_tok[0:n, t % 2, D:D + 64], normed[0:n, t % 2, 128:D],
                                  split_f[0:n, t % 2, 128:D], ALU.subtract)
                dve.tensor_tensor(split_tok[0:n, t % 2, D + 64:2 * D], normed[0:n, t % 2, 0:128],
                                  split_f[0:n, t % 2, 0:128], ALU.subtract).then_inc(s_tok_lo, 1)

            dve.wait_ge(s_first, 16)
            for t, (a, n) in enumerate(TILES):
                dve.scalar_tensor_tensor(out=base[0:n, t, :], in0=col("b")[0:n, :],
                                         scalar=col("token_is_patch")[0:n, t:t + 1], in1=base[0:n, t, :],
                                         op0=ALU.mult, op1=ALU.add).then_inc(s_base, 1)
            dve.wait_ge(s_base, NT)
            for t in range(NT + 2):
                if t < NT:
                    n = TILES[t][1]
                    dve.wait_ge(s_embed, t + 1)
                    dve.tensor_tensor(h_tok[0:n, t, :], ps[0:n, t % 2, 0:D], base[0:n, t, :], ALU.add).then_inc(s_h, 1)
                    dve.wait_ge(s_h, t + 1)
                    moments(t, h_tok)
                if 1 <= t <= NT:
                    normalize(t - 1, h_tok)
                if t >= 2:
                    low_of(t - 2)

            for u in range(4):
                j, m = u // 2, u % 2
                dve.wait_ge(s_k, u + 1)
                dve.tensor_reduce(sums[:, 0, j, m, :],
                                  ps[0:HALF_D, 4 + u % 2, 0:HALF_I * EVEN].rearrange("p (i t) -> p i t", t=EVEN)[:, :, 0:TOK],
                                  AX.X, ALU.add, apply_absolute_value=True).then_inc(s_k_used, 1)
                dve.wait_ge(s_k_used, u + 1)
                dve.wait_ge(s_q, u + 1)
                q = ps[0:HALF_D, 6 + u % 2, 0:HALF_I * EVEN].rearrange("p (i t) -> p i t", t=EVEN)[:, :, 0:TOK]
                link(dve.tensor_reduce(sums[:, 1, j, m, :], q, AX.X, ALU.add, apply_absolute_value=True))
                link(dve.tensor_scalar(sums[:, :, j, m, :], sums[:, :, j, m, :], L1_EPS, None, ALU.max))
                link(dve.reciprocal(sums[:, :, j, m, :], sums[:, :, j, m, :]))
                link(dve.tensor_tensor(scale_qk[:, j, m, :], sums[:, 0, j, m, :], sums[:, 1, j, m, :], ALU.mult))
                dve.tensor_tensor(qT[:, m, HALF_T * j:HALF_T * (j + 1)].rearrange("p (i t) -> p i t", t=TOK), q,
                                  scale_qk[:, j, m, :].unsqueeze(2).broadcast_to([HALF_D, HALF_I, TOK]),
                                  ALU.mult).then_inc(s_q_used, 1)
            dve.wait_ge(s_small, 16)
            for p in range(PAIRS):
                dve.wait_ge(s_outer, p + 1)
                b = 2 + 2 * (p % 2)
                dve.tensor_tensor(kv_blocks[:, 2 * p:2 * p + 2, :], ps[0:HALF_D, b:b + 2, 0:D],
                                  col("blocks")[0:HALF_D, :].unsqueeze(1).broadcast_to([HALF_D, 2, D]),
                                  ALU.mult).then_inc(s_blocks, 1)
            for t in range(NT + 2):
                if t < NT:
                    n = TILES[t][1]
                    dve.wait_ge(s_proj, t + 1)
                    dve.wait_ge(s_hb, t + 1)
                    dve.tensor_tensor(h2_tok[0:n, t, :], ps[0:n, t % 2, 0:D], h2_tok[0:n, t, :],
                                      ALU.add).then_inc(s_h2, 1)
                    dve.wait_ge(s_h2, t + 1)
                    moments(NT + t, h2_tok)
                if 1 <= t <= NT:
                    normalize(NT + t - 1, h2_tok)
                if t >= 2:
                    low_of(NT + t - 2)

            def take_prod(u):
                m, j = UNITS[u]
                r = rows_of(m)
                dve.wait_ge(s_up, u + 1)
                dve.wait_ge(s_silu, u + 1)
                dve.scalar_tensor_tensor(out=prod[0:r, u % T_SLOTS, :], in0=ps[0:r, 2 + u % 2, 0:HALF_T],
                                         scalar=col("up_b")[0:r, m:m + 1], in1=silu_g[0:r, u % S_SLOTS, :],
                                         op0=ALU.add, op1=ALU.mult).then_inc(s_prod, 1)

            def weigh(u):
                m, j = UNITS[u]
                r = rows_of(m)
                dve.wait_ge(s_prod, u + 1)
                if u >= H_SLOTS:
                    dve.wait_ge(s_hid_lo, u - H_SLOTS + 1)
                if m >= SHARED_MB:
                    dve.wait_ge(s_spread_ps, u - 2 * SHARED_MB + 1)
                    dve.tensor_tensor(hid[0:r, u % H_SLOTS, :], prod[0:r, u % T_SLOTS, :],
                                      ps[0:r, 7, 0:HALF_T], ALU.mult).then_inc(s_hid, 1)
                else:
                    dve.tensor_copy(hid[0:r, u % H_SLOTS, :], prod[0:r, u % T_SLOTS, :]).then_inc(s_hid, 1)

            def group_scores():
                c = choice[:, :, :].rearrange("p t (g e) -> p (t g) e", e=PER_GROUP)
                dve.tensor_tensor(pair_sums[:, :, 0:2], c[:, :, 0:2], c[:, :, 2:4], ALU.add)
                dve.tensor_tensor(pair_sums[:, :, 2:4], c[:, :, 0:4:2], c[:, :, 1:4:2], ALU.add)
                dve.tensor_tensor(pair_sums[:, :, 4:5], c[:, :, 0:1], c[:, :, 3:4], ALU.add)
                link(dve.tensor_tensor(pair_sums[:, :, 5:6], c[:, :, 1:2], c[:, :, 2:3], ALU.add))
                link(dve.tensor_reduce(group_s[:, :, :], pair_sums[:, :, :], AX.X, ALU.max))

            def group_ranks():
                for i, (op, order) in enumerate(((ALU.is_ge, "before"), (ALU.is_gt, "after"))):
                    out4 = beaten[:, i, :, :].rearrange("p t (g o) -> p t g o", o=GROUPS)
                    link(dve.tensor_tensor(out4, group_s[:, :, :].unsqueeze(2).broadcast_to([128, NT, GROUPS, GROUPS]),
                                           group_s[:, :, :].unsqueeze(3).broadcast_to([128, NT, GROUPS, GROUPS]), op))
                    link(dve.tensor_tensor(beaten[:, i, :, :], beaten[:, i, :, :],
                                           col(order).unsqueeze(1).broadcast_to([128, NT, GROUPS * GROUPS]), ALU.mult))
                link(dve.tensor_tensor(beaten[:, 0, :, :], beaten[:, 0, :, :], beaten[:, 1, :, :], ALU.add))
                link(dve.tensor_reduce(rank[:, :, :], beaten[:, 0, :, :].rearrange("p t (g o) -> p t g o", o=GROUPS),
                                       AX.X, ALU.add))
                link(dve.tensor_scalar(rank[:, :, :], rank[:, :, :], TOP_GROUPS - 0.5, None, ALU.is_lt))

            def expert_choice():
                g = rank[:, :, :].unsqueeze(3).broadcast_to([128, NT, GROUPS, PER_GROUP])
                link(dve.tensor_tensor(choice[:, :, :].rearrange("p t (g e) -> p t g e", e=PER_GROUP),
                                       choice[:, :, :].rearrange("p t (g e) -> p t g e", e=PER_GROUP), g, ALU.mult))
                link(dve.tensor_scalar(masked[:, :, 0:EXPERTS], choice[:, :, :], 0.0, None, ALU.add))
                for t in range(NT):
                    ins = dve.max(top8[:, t, :], masked[:, t, 0:EXPERTS])
                link(ins)
                link(dve.tensor_copy(taken8[:, :, 0:TOP_K], top8[:, :, 0:TOP_K]))
                for t in range(NT):
                    ins = dve.match_replace(marked[:, t, :], taken8[:, t, :], masked[:, t, :], TAKEN)
                link(ins)

            def combine_weights():
                link(dve.scalar_tensor_tensor(out=weight[:, :, :], in0=marked[:, :, 0:EXPERTS], scalar=TAKEN,
                                              in1=scores[:, :, :], op0=ALU.is_equal, op1=ALU.mult))
                link(dve.tensor_reduce(w_sum[:, 0, :], weight[:, :, :], AX.X, ALU.add))
                link(dve.tensor_scalar(w_sum[:, 1, :], w_sum[:, 0, :], SUM_EPS, None, ALU.add))
                link(dve.reciprocal(w_sum[:, 2, :], w_sum[:, 1, :]))
                link(dve.scalar_tensor_tensor(out=combine[:, :, :], in0=weight[:, :, :], scalar=SCALE,
                                              in1=w_sum[:, 2, :].unsqueeze(2).broadcast_to([128, NT, EXPERTS]),
                                              op0=ALU.mult, op1=ALU.mult))
                link(dve.tensor_copy(combine_split[:, :, 0:EXPERTS], combine[:, :, :]))
                dve.tensor_tensor(combine_split[:, :, EXPERTS:2 * EXPERTS], combine[:, :, :],
                                  combine_split_f[:, :, 0:EXPERTS], ALU.subtract).then_inc(s_combine, 1)

            dve.wait_ge(s_zero, 1)
            dve.wait_ge(s_logits_ps, NT)
            full = NT - 1
            n = TILES[full][1]
            rb = col("router_b")
            link(dve.tensor_tensor(logits[:, 0:full, :],
                                   ps[:, 4, 0:EXPERTS * full].rearrange("p (t e) -> p t e", e=EXPERTS),
                                   rb.unsqueeze(1).broadcast_to([128, full, EXPERTS]), ALU.add))
            dve.tensor_tensor(logits[0:n, full, :], ps[0:n, 4, EXPERTS * full:EXPERTS * NT], rb[0:n, :],
                              ALU.add).then_inc(s_logits, 1)
            dve.wait_ge(s_scores, 1)
            link(dve.tensor_tensor(choice[:, :, :], scores[:, :, :],
                                   col("corr").unsqueeze(1).broadcast_to([128, NT, EXPERTS]), ALU.add))
            group_scores()
            take_prod(0)
            group_ranks()
            take_prod(1)
            expert_choice()
            take_prod(2)
            combine_weights()
            take_prod(3)
            for u in range(4, ROUTE_AT):
                take_prod(u)
                if u - LAG < 2 * SHARED_MB:
                    weigh(u - 4)
            dve.wait_ge(s_combine_ps, 1)
            dve.tensor_copy(combineT[:, 0:512], ps[0:CROWS, 7, 0:512]).then_inc(s_combineT, 1)
            dve.tensor_copy(combineT[:, 512:T], ps[0:CROWS, 6, 0:T - 512]).then_inc(s_combineT, 1)
            for u in range(ROUTE_AT - 4, 2 * SHARED_MB):
                weigh(u)
            for u in range(ROUTE_AT, NU + LAG):
                if u < NU:
                    take_prod(u)
                weigh(u - LAG)

            for t, (a, n) in enumerate(TILES):
                dve.wait_ge(s_down, min(NT, t // 2 * 2 + 2))
                if t >= 2:
                    dve.wait_ge(s_stored[t % 2], 16 * (t // 2))
                dve.tensor_tensor(out_tok[0:n, t % 2, :], ps[0:n, 4 + t // 2, D * (t % 2):D * (t % 2 + 1)],
                                  h2_tok[0:n, t, :],
                                  ALU.add).then_inc(s_out_tok, 1)


def kernel(**inputs):
    import concourse.bacc as _bacc
    from concourse.bass_utils import run_bass_kernel_spmd as _run

    g = {k.replace("L0_", ""): np.asarray(v) for k, v in inputs.items()}
    f = np.float32

    def rows128(a):
        k = -(-a.shape[0] // 128)
        full = np.zeros((k * 128, a.shape[1]), f)
        full[:a.shape[0]] = a
        return full.reshape(k, 128, -1).transpose(1, 0, 2)

    def blocks128(shared, routed):
        return np.concatenate([rows128(shared), rows128(routed)], axis=1)

    x = g["x"].reshape(IMAGES, CHANNELS, GRID, PATCH, GRID, PATCH).transpose(1, 3, 5, 0, 2, 4)
    cols = np.zeros((CHANNELS * PATCH * PATCH, IMAGES, TOK), f)
    cols[:, :, 1:] = x.reshape(-1, IMAGES, GRID * GRID)
    cols = rows128(cols.reshape(-1, T))
    patches = np.concatenate([cols[:, :, a:a + n].reshape(128, -1) for a, n in TILES], axis=1)

    near = np.arange(GRID) * POS_SIDE // GRID
    pos = g["tok_positions"][0][:, near][:, :, near].reshape(D, -1).T
    base = np.concatenate([g["tok_cls_embedding"].reshape(1, D), pos])
    small = np.zeros((128, SMALL_COLS), f)

    def put(name, a, rows=128):
        lo, hi = COLS[name]
        small[:rows, lo:hi] = a

    put("ident", np.eye(128, dtype=f))
    put("token_is_patch", rows128((np.arange(T) % TOK > 0).astype(f)[:, None])[:, :, 0])
    put("b", g["tok_b"][None])
    put("base", rows128(np.tile(base, (IMAGES, 1))).reshape(128, -1))
    put("patch_w", rows128(g["tok_W"]).reshape(128, -1))
    heads = np.arange(HALF_D) // HEAD
    put("blocks", np.tile((heads[:, None] == heads).astype(f), (1, 2)), HALF_D)
    put("b_proj", g["attn_b_proj"][None])
    put("w_proj", g["attn_w_proj"].T.reshape(2, HALF_D, D).transpose(1, 0, 2).reshape(HALF_D, -1), HALF_D)
    put("router_b", g["ffn_router_b"][None])
    put("corr", g["ffn_corr_bias"][None])
    k = np.arange(GROUPS)
    put("before", (k < k[:, None]).astype(f).reshape(1, -1))
    put("after", (k > k[:, None]).astype(f).reshape(1, -1))
    for name, routed, shared in (("gate_b", "gbg", "sbg"), ("up_b", "gbu", "sbu")):
        put(name, blocks128(g[f"ffn_{shared}"][:, None], g[f"ffn_{routed}"].reshape(-1, 1))[:, :, 0])

    def x_side(w):
        return np.stack([w[:128], np.concatenate([w[128:], w[128:]])], axis=1)

    x_w = x_side(np.concatenate([g["attn_w_qkv"].T, g["ffn_router_w"].T], axis=1))
    gate, up = (x_side(np.concatenate([g[f"ffn_{s}"], g[f"ffn_{r}"].transpose(1, 0, 2).reshape(D, ROUTED)], axis=1))
                for r, s in (("gWg", "sWg"), ("gWu", "sWu")))
    moe_w = np.zeros((128, MB, 512), f)
    for m, (a, n) in enumerate(BLOCKS):
        moe_w[:, m, :4 * n] = np.concatenate([w[:, :, a:a + n].reshape(128, -1) for w in (gate, up)], axis=1)
    moe_w = moe_w.reshape(128, -1)
    down_w = blocks128(g["ffn_sWd"], g["ffn_gWd"].reshape(ROUTED, D))
    down_b = np.concatenate([g["ffn_gbd"], g["ffn_gbd"], g["ffn_sbd"][None]])
    of = (np.arange(ROUTED) // INNER == np.arange(EXPERTS)[:, None]).astype(f)
    spread = np.concatenate([of, of, np.zeros((1, ROUTED), f)])

    nc = _bacc.Bacc("TRN2", target_bir_lowering=False, num_devices=1)
    arrays, args = {}, []
    for name, a in (("patches", patches), ("small", small), ("x_w", x_w), ("moe_w", moe_w), ("down_w", down_w),
                    ("down_b", down_b), ("spread", spread)):
        a = np.ascontiguousarray(a)
        arrays[f"in_{name}"] = a
        args.append(nc.dram_tensor(f"in_{name}", a.shape, mybir.dt.from_np(a.dtype), kind="ExternalInput").ap())
    args.append(nc.dram_tensor("out_tokens", (T, D), mybir.dt.float32, kind="ExternalOutput").ap())
    tower(nc, *args)
    r = _run(nc, [arrays], core_ids=[0])
    return r.results[0]["out_tokens"].reshape(IMAGES, TOK, D)
```

```python
import numpy as np
import concourse.bass as bass
from concourse import mybir
from contextlib import ExitStack

IMAGES, CHANNELS, SIDE, PATCH = 16, 3, 96, 16
GRID = SIDE // PATCH
POS_SIDE = 14
D = 192
TOK = GRID * GRID + 1
T = IMAGES * TOK
TILES = [(t, min(128, T - t)) for t in range(0, T, 128)]
NT = len(TILES)
PATCH_K = CHANNELS * PATCH * PATCH // 128
HEAD, HALF_D = 16, D // 2
SLOT = 64
EVEN = TOK + 1
HALF_T = T // 2
HALF_I = IMAGES // 2
PAIRS = IMAGES // 2
EXPERTS, GROUPS, INNER = 16, 4, 96
PER_GROUP = EXPERTS // GROUPS
TOP_GROUPS, TOP_K, SCALE = 2, 4, 2.5
ROUTED, SHARED = EXPERTS * INNER, 2 * INNER
HID = ROUTED + SHARED
BLOCKS = [(a, min(128, SHARED - a)) for a in range(0, SHARED, 128)]
SHARED_MB = len(BLOCKS)
BLOCKS += [(a, 128) for a in range(SHARED, HID, 128)]
MB = len(BLOCKS)
PARTS = [(0, 2 * 128), (2 * 128, T - 2 * 128)]
PART_MAX = max(n for _, n in PARTS)
EARLY = 5
UNITS = [(m, j) for j in range(2) for m in range(EARLY)] + [(m, j) for m in range(EARLY, MB) for j in range(2)]
NU = len(UNITS)
LN_EPS, L1_EPS, SUM_EPS = 1e-5, 1e-12, 1e-20
XW = 3 * D + EXPERTS
CROWS = 2 * EXPERTS + 1
PAD, TAKEN = -3e38, 3e38


def rows_of(m):
    return BLOCKS[m][1]


_at = 0
COLS = {}
for _name, _n in (("ident", 128), ("token_is_patch", NT), ("b", D), ("base", NT * D), ("blocks", D), ("b_proj", D), ("w_proj", 2 * D), ("router_b", 1), ("corr", EXPERTS),
                  ("before", GROUPS * GROUPS), ("after", GROUPS * GROUPS), ("gate_b", MB), ("up_b", MB)):
    COLS[_name] = (_at, _at + _n)
    _at += _n
FIRST_COLS = COLS["blocks"][0]
SMALL_COLS = _at

CHUNK = 2
CHUNKS = MB // CHUNK
RAW_SLOTS = 3
ROUTE_AT, LAG = 12, 2
WEIGHED = [u for u in range(NU) if UNITS[u][0] < SHARED_MB] + [u for u in range(NU) if UNITS[u][0] >= SHARED_MB]
N_SHARED_UNITS = 2 * SHARED_MB
FIRST_OF, LAST_OF = ([WEIGHED.index(UNITS.index((m, j))) for m in range(MB)] for j in range(2))
BY_POOL = list(range(6, 13))
FIRST_SPLITS = 6
SPLIT_AT = {}
for _m in range(FIRST_SPLITS, 14):
    SPLIT_AT[2 * (_m - FIRST_SPLITS)] = _m
DOWN_SPLITS = 4


def by_vector(u):
    return u + 1 - sum(p <= u for p in BY_POOL)


def steps():
    at, step, w = [], 0, 0
    while w < NU:
        now = []
        while w < NU and len(now) < 2 and WEIGHED[w] <= step - LAG and (w < N_SHARED_UNITS or step >= ROUTE_AT):
            now.append(w)
            w += 1
        at.append(now)
        step += 1
    when = {w: s for s, now in enumerate(at) for w in now}
    down = {}
    for m in range(MB):
        for tiles, w in (((0, 1), FIRST_OF[m]), ((2, 3, 4), LAST_OF[m])) if m == MB - 1 else ((range(NT), LAST_OF[m]),):
            down.setdefault(max(when[w] + 2, ROUTE_AT + m), []).append((m, list(tiles)))
    return at, down


WEIGH_AT, DOWN_AT = steps()
STEPS = max(DOWN_AT) + 1
WEIGH_AT += [[]] * (STEPS - len(WEIGH_AT))
MOE_SLOTS = 8
T_SLOTS, S_SLOTS, H_SLOTS, BLOCK_SLOTS = 12, 2, 3, 3


def tower(nc, patches, patch_w_in, small, x_w, moe_w, down_w, down_b, spread, out):
    dt = mybir.dt
    f32, f32r = dt.float32, dt.float32r
    ALU = mybir.AluOpType
    ACT = mybir.ActivationFunctionType
    AX = mybir.AxisListType

    with ExitStack() as ctx:
        def sb(name, shape, t=f32):
            return ctx.enter_context(nc.sbuf_tensor(name, shape, t))

        def sem(name):
            return ctx.enter_context(nc.semaphore(name))

        patch_sb = sb("patch_sb", [128, PATCH_K * (T + D)])
        small_sb = sb("small_sb", [128, SMALL_COLS])
        xw_raw = sb("xw_raw", [128, 2, XW])
        moe_raw = sb("moe_raw", [128, RAW_SLOTS, CHUNK * 512])
        down_raw = patch_sb[:, 0:MB * D].rearrange("p (m d) -> p m d", d=D)
        down_b_raw = sb("down_b_raw", [CROWS, D])
        spread_raw = patch_sb[0:CROWS, MB * D:MB * D + ROUTED]
        xw_hi = sb("xw_hi", [128, 2, XW], f32r)
        xw_lo = sb("xw_lo", [128, 2, XW], f32r)
        moe_hi = sb("moe_hi", [128, MOE_SLOTS, 512], f32r)
        moe_lo = sb("moe_lo", [128, MOE_SLOTS, 512], f32r)
        down_hi = sb("down_hi", [128, MB, D], f32r)
        down_lo = sb("down_lo", [128, MB, D], f32r)
        down_b_hi = sb("down_b_hi", [CROWS, D], f32r)
        down_b_lo = sb("down_b_lo", [CROWS, D], f32r)
        spread_sb = sb("spread_sb", [CROWS, ROUTED], f32r)
        h_tok = sb("h_tok", [128, NT, D])
        h2_tok = sb("h2_tok", [128, NT, D])
        stats = sb("stats", [128, 2, 6])
        mean_var = sb("mean_var", [128, 2 * NT, 2])
        root = sb("root", [128, 2 * NT, 6])
        normed = sb("normed", [128, 3, D])
        split_tok = sb("split_tok", [128, 3, 2 * D], f32r)
        out_tok = sb("out_tok", [128, 2, D])
        x1T = sb("x1T", [128, 3, IMAGES, SLOT], f32r)
        x2T = x1T[:, :, :, :].rearrange("p i m t -> p i (m t)")[:, :, 0:T]
        sums = sb("sums", [HALF_D, 2, 2, 2, HALF_I])
        scale_qk = sb("scale_qk", [HALF_D, 2, 2, HALF_I])
        kv_tok = sb("kv_tok", [128, 4, 2 * D])
        wide = sb("wide", [128, max(IMAGES * D + 2 * T, T_SLOTS * PART_MAX)])
        kv_blocks = wide[0:HALF_D, 0:IMAGES * D].rearrange("p (i d) -> p i d", d=D)
        qT = wide[0:HALF_D, IMAGES * D:IMAGES * D + 2 * T].rearrange("p (m t) -> p m t", t=T)
        prod = wide[:, 0:T_SLOTS * PART_MAX].rearrange("p (s t) -> p s t", t=PART_MAX)
        attn_hi = sb("attn_hi", [HALF_D, 2, T], f32r)
        attn_lo = sb("attn_lo", [HALF_D, 2, T], f32r)
        w_proj_hi = sb("w_proj_hi", [HALF_D, 2, D], f32r)
        w_proj_lo = sb("w_proj_lo", [HALF_D, 2, D], f32r)
        scoresT = sb("scoresT", [EXPERTS, T])
        scores = sb("scores", [128, NT, EXPERTS])
        choice = sb("choice", [128, NT, EXPERTS])
        pair_sums = sb("pair_sums", [128, NT * GROUPS, 6])
        group_s = sb("group_s", [128, NT, GROUPS])
        beaten = sb("beaten", [128, 2, NT, GROUPS * GROUPS])
        rank = sb("rank", [128, NT, GROUPS])
        masked = sb("masked", [128, NT, EXPERTS + TOP_K])
        top8 = sb("top8", [128, NT, 8])
        taken8 = sb("taken8", [128, NT, 8])
        marked = sb("marked", [128, NT, EXPERTS + TOP_K])
        weight = sb("weight", [128, NT, EXPERTS])
        w_sum = sb("w_sum", [128, 3, NT])
        combine = sb("combine", [128, NT, EXPERTS])
        combine_split = sb("combine_split", [128, NT, CROWS], f32r)
        combineT = sb("combineT", [CROWS, T], f32r)
        sig_g = sb("sig_g", [128, S_SLOTS, PART_MAX])
        up_b = sb("up_b", [128, 2, PART_MAX])
        hid = xw_raw[:, :, :].rearrange("p i n -> p (i n)")[:, 0:H_SLOTS * PART_MAX].rearrange("p (s t) -> p s t", t=PART_MAX)
        hid_hi = sb("hid_hi", [128, BLOCK_SLOTS, T], f32r)
        hid_lo = sb("hid_lo", [128, BLOCK_SLOTS, T], f32r)

        ps = ctx.enter_context(nc.psum_tensor("ps", [128, 8, 512], f32))

        def col(name):
            a, b = COLS[name]
            return small_sb[:, a:b]

        ident = col("ident")
        base = col("base").rearrange("p (t d) -> p t d", d=D)
        patch_w = patch_sb[:, PATCH_K * T:PATCH_K * (T + D)].rearrange("p (k d) -> p k d", d=D)
        w_proj = col("w_proj").rearrange("p (m d) -> p m d", d=D)
        split_f = split_tok[:, :, :].bitcast(f32)
        combine_split_f = combine_split[:, :, :].bitcast(f32)

        s_patch = [sem(f"s_patch{t}") for t in range(NT)]
        s_patch_w = [sem(f"s_patch_w{i}") for i in range(2)]
        s_first, s_small, s_xw, s_consts = sem("s_first"), sem("s_small"), sem("s_xw"), sem("s_consts")
        s_moe_in = [sem(f"s_moe_in{i}") for i in range(RAW_SLOTS)]
        s_down_in = sem("s_down_in")
        s_moe_hi, s_moe_lo = sem("s_moe_hi"), sem("s_moe_lo")
        s_xw_hi, s_xw_lo = sem("s_xw_hi"), sem("s_xw_lo")
        s_down_hi, s_down_lo = sem("s_down_hi"), sem("s_down_lo")
        s_spread = sem("s_spread")
        s_zero = sem("s_zero")
        s_base = sem("s_base")
        s_embed = sem("s_embed")
        s_var = sem("s_var")
        s_root = sem("s_root")
        s_normed = sem("s_normed")
        s_tok_hi, s_tok_lo = sem("s_tok_hi"), sem("s_tok_lo")
        s_turned = sem("s_turned")
        s_xT = sem("s_xT")
        s_k, s_q = sem("s_k"), sem("s_q")
        s_qk_summed, s_q_copied, s_scale, s_qT = sem("s_qk_summed"), sem("s_q_copied"), sem("s_scale"), sem("s_qT")
        s_w_proj_hi, s_w_proj_lo = sem("s_w_proj_hi"), sem("s_w_proj_lo")
        s_kv, s_kv_tok = sem("s_kv"), sem("s_kv_tok")
        s_outer, s_blocks = sem("s_outer"), sem("s_blocks")
        s_attn, s_attn_hi, s_attn_lo = sem("s_attn"), sem("s_attn_hi"), sem("s_attn_lo")
        s_hb = sem("s_hb")
        s_h = sem("s_h")
        s_proj = sem("s_proj")
        s_h2 = sem("s_h2")
        s_logits, s_scoresT, s_scores_ps, s_scores = sem("s_logits"), sem("s_scoresT"), sem("s_scores_ps"), sem("s_scores")
        s_combine, s_combine_ps, s_combineT = sem("s_combine"), sem("s_combine_ps"), sem("s_combineT")
        s_gate, s_up, s_spread_ps = sem("s_gate"), sem("s_up"), sem("s_spread_ps")
        s_sig, s_gated, s_prod, s_hid = sem("s_sig"), sem("s_gated"), sem("s_prod"), sem("s_hid")
        s_hid_hi, s_hid_lo = sem("s_hid_hi"), sem("s_hid_lo")
        s_up_copied, s_prod_pool = sem("s_up_copied"), sem("s_prod_pool")
        s_block_down = sem("s_block_down")
        s_down, s_out_tok = sem("s_down"), sem("s_out_tok")
        s_stored = [sem(f"s_stored{i}") for i in range(2)]
        s_dve, s_pool = sem("s_dve"), sem("s_pool")

        block = ctx.enter_context(nc.Block())

        @block.sync
        def _(sp):
            def load_small(a, b, sem_):
                sp.dma_start(small_sb[:, a:b], small[:, a:b]).then_inc(sem_, 16)

            def load_patches(t):
                a, n = TILES[t]
                sp.dma_start(patch_sb[:, PATCH_K * a:PATCH_K * (a + n)],
                             patches[:, PATCH_K * a:PATCH_K * (a + n)]).then_inc(s_patch[t], 16)

            half_w = PATCH_K * D // 2
            def load_patch_w(i):
                sp.dma_start(patch_sb[:, PATCH_K * T + half_w * i:PATCH_K * T + half_w * (i + 1)],
                             patch_w_in[:, half_w * i:half_w * (i + 1)]).then_inc(s_patch_w[i], 16)

            load_patch_w(0)
            load_patches(0)
            load_patch_w(1)
            load_patches(1)
            load_small(0, FIRST_COLS, s_first)
            load_patches(2)
            sp.dma_start(xw_raw[:, :, :], x_w).then_inc(s_xw, 16)
            load_patches(3)
            load_patches(4)
            load_small(FIRST_COLS, SMALL_COLS, s_small)
            for c in range(CHUNKS):
                if c >= RAW_SLOTS:
                    sp.wait_ge(s_moe_hi, CHUNK * (c - RAW_SLOTS + 1))
                    sp.wait_ge(s_moe_lo, CHUNK * (c - RAW_SLOTS + 1))
                a = 512 * CHUNK * c
                sp.dma_start(moe_raw[:, c % RAW_SLOTS, :], moe_w[:, a:a + 512 * CHUNK]).then_inc(s_moe_in[c % RAW_SLOTS], 16)
                if c == RAW_SLOTS - 1:
                    sp.dma_start(down_b_raw[:, :], down_b).then_inc(s_consts, 16)
                    sp.wait_ge(s_embed, NT)
                    sp.dma_start(spread_raw, spread).then_inc(s_consts, 16)
                    sp.dma_start(down_raw, down_w).then_inc(s_down_in, 16)
            for t, (a, n) in enumerate(TILES):
                sp.wait_ge(s_out_tok, t + 1)
                sp.dma_start(out[a:a + n, :], out_tok[0:n, t % 2, :]).then_inc(s_stored[t % 2], 16)
            for i in range(2):
                sp.wait_ge(s_stored[i], 16 * len(range(i, NT, 2)))

        turn_bank = [2, 3, 2, 3, 2] + [2, 3, 4, 5, 6]
        proj_bank = [6, 7, 0, 1, 4]

        @block.tensor
        def _(pe):
            def product(o, hi, lo, x, tokens_are_weights=False):
                terms = ((hi[0], 0), (lo[0], 0), (hi[0], 2), (hi[1], 1), (lo[1], 1))
                for i, (w, part) in enumerate(terms):
                    a, b = (x(part), w) if tokens_are_weights else (w, x(part))
                    last = pe.matmul(o, a, b, start=(i == 0), stop=(i == len(terms) - 1))
                return last

            def x_weights(a, b):
                return [xw_hi[:, i, a:b] for i in range(2)], [xw_lo[:, i, a:b] for i in range(2)]

            def embed(t):
                a, n = TILES[t]
                pe.wait_ge(s_patch[t], 16)
                if t >= 2:
                    pe.wait_ge(s_h, t - 1)
                tile = patch_sb[:, PATCH_K * a:PATCH_K * (a + n)].rearrange("p (k t) -> p k t", k=PATCH_K)
                for k in range(PATCH_K):
                    if t == 0 and k % (PATCH_K // 2) == 0:
                        pe.wait_ge(s_patch_w[k // (PATCH_K // 2)], 16)
                    last = pe.matmul(ps[0:n, t % 2, 0:D], tile[:, k, :], patch_w[:, k, :],
                                     start=(k == 0), stop=(k == PATCH_K - 1))
                last.then_inc(s_embed, 1)

            def turn(t):
                a, n = TILES[t % NT]
                if t == 0:
                    pe.wait_ge(s_first, 16)
                pe.wait_ge(s_tok_hi, t + 1)
                pe.wait_ge(s_tok_lo, t + 1)
                if t == NT + 2:
                    pe.wait_ge(s_h2, NT)
                if 2 <= t < NT:
                    pe.wait_ge(s_xT, t - 1)
                for i in range(3):
                    last = pe.transpose(ps[:, turn_bank[t], 128 * i:128 * i + n],
                                        split_f[0:n, t % 3, 128 * i:128 * i + 128], ident[0:n, 0:n])
                last.then_inc(s_turned, 1)

            def qk(j):
                pe.wait_ge(s_xT, 3 if j == 0 else NT)
                if j == 0:
                    pe.wait_ge(s_xw_hi, 1)
                    pe.wait_ge(s_xw_lo, 1)
                    pe.wait_ge(s_zero, 1)
                else:
                    pe.wait_ge(s_qk_summed, 4)
                    pe.wait_ge(s_q_copied, 2)
                im = slice(HALF_I * j, HALF_I * (j + 1))
                for kind, done, bank in ((1, s_k, 4), (0, s_q, 6)):
                    for m in range(2):
                        c = D * kind + HALF_D * m
                        product(ps[0:HALF_D, bank + m, 0:HALF_I * EVEN], *x_weights(c, c + HALF_D),
                                lambda i: x1T[:, i, im, 0:EVEN]).then_inc(done, 1)

            def kv(p):
                if p == 0:
                    pe.wait_ge(s_h, NT)
                if p == 4:
                    pe.wait_ge(s_xT, NT)
                if p >= 2:
                    pe.wait_ge(s_kv_tok, p - 1)
                product(ps[:, p % 2, 0:2 * D], *x_weights(D, 3 * D),
                        lambda i: x1T[:, i, 2 * p:2 * p + 2, :].rearrange("p m t -> p (m t)"), True).then_inc(s_kv, 1)

            def outer(p):
                pe.wait_ge(s_kv_tok, p + 1)
                if p >= 2:
                    pe.wait_ge(s_blocks, p - 1)
                if p == 0:
                    pe.wait_ge(s_xT, NT)
                if p == 1:
                    pe.wait_ge(s_qk_summed, 8)
                for m in range(2):
                    for i in range(2):
                        r = slice(64 * i, 64 * i + TOK)
                        last = pe.matmul(ps[0:HALF_D, 2 + 2 * (p % 2) + i, HALF_D * m:HALF_D * (m + 1)],
                                         kv_tok[r, p % 4, HALF_D * m:HALF_D * (m + 1)],
                                         kv_tok[r, p % 4, D + HALF_D * m:D + HALF_D * (m + 1)],
                                         start=True, stop=True)
                last.then_inc(s_outer, 1)

            def attend(j, m):
                pe.wait_ge(s_qT, 2 * (j + 1))
                pe.wait_ge(s_blocks, PAIRS // 2 * (j + 1))
                if j == 0:
                    pe.wait_ge(s_qk_summed, 8)
                    pe.wait_ge(s_q_copied, 4)
                else:
                    pe.wait_ge(s_h2, m + 1)
                for i in range(HALF_I):
                    im = HALF_I * j + i
                    last = pe.matmul(ps[0:HALF_D, 6 + m, TOK * i:TOK * (i + 1)],
                                     kv_blocks[:, im, HALF_D * m:HALF_D * (m + 1)],
                                     qT[:, m, TOK * im:TOK * (im + 1)], start=True, stop=True)
                last.then_inc(s_attn, 1)

            def project(t):
                a, n = TILES[t]
                half = 1 if a + n <= HALF_T else 2
                pe.wait_ge(s_attn_hi, 2 * half)
                pe.wait_ge(s_attn_lo, 2 * half)
                if t == 0:
                    pe.wait_ge(s_w_proj_hi, 1)
                    pe.wait_ge(s_w_proj_lo, 1)
                if t == 2:
                    pe.wait_ge(s_kv_tok, PAIRS)
                terms = [(x, w, m) for x, w in ((attn_hi, w_proj_hi), (attn_hi, w_proj_lo), (attn_lo, w_proj_hi))
                         for m in range(2)]
                for i, (x, w, m) in enumerate(terms):
                    last = pe.matmul(ps[0:n, proj_bank[t], 0:D], x[:, m, a:a + n], w[:, m, :],
                                     start=(i == 0), stop=(i == len(terms) - 1))
                last.then_inc(s_proj, 1)

            def router(j):
                a, n = PARTS[j]
                pe.wait_ge(s_xT, NT + 2 if j == 0 else 2 * NT)
                pe.wait_ge(s_attn_lo, 4)
                product(ps[0:EXPERTS, 7 if j == 0 else 4, 0:n], *x_weights(3 * D, XW),
                        lambda i: x2T[:, i, a:a + n]).then_inc(s_logits, 1)

            def turn_scores():
                pe.wait_ge(s_scoresT, 2)
                for t, (a, n) in enumerate(TILES):
                    last = pe.transpose(ps[0:n, 5, EXPERTS * t:EXPERTS * (t + 1)], scoresT[:, a:a + n],
                                        ident[0:EXPERTS, 0:EXPERTS])
                last.then_inc(s_scores_ps, 1)

            def hidden(u, at, bank, done):
                m, j = UNITS[u]
                a, n = PARTS[j]
                r = rows_of(m)
                at *= r
                hi, lo = moe_hi[:, m % MOE_SLOTS, :], moe_lo[:, m % MOE_SLOTS, :]
                product(ps[0:r, bank + u % 2, 0:n],
                        [hi[:, at:at + r], hi[:, at + r:at + 2 * r]], [lo[:, at:at + r], lo[:, at + r:at + 2 * r]],
                        lambda i: x2T[:, i, a:a + n]).then_inc(done, 1)

            def gate(u):
                m, j = UNITS[u]
                pe.wait_ge(s_moe_hi, m + 1)
                pe.wait_ge(s_moe_lo, m + 1)
                if u == 0:
                    pe.wait_ge(s_xT, NT + 2)
                if u < 2:
                    pe.wait_ge(s_h2, u + 3)
                if j == 1:
                    pe.wait_ge(s_xT, 2 * NT)
                if u >= 2:
                    pe.wait_ge(s_gated, u - 1)
                hidden(u, 0, 0, s_gate)

            def up(u):
                if u >= 2:
                    if u - 2 in BY_POOL:
                        pe.wait_ge(s_up_copied, BY_POOL.index(u - 2) + 1)
                    else:
                        pe.wait_ge(s_prod, by_vector(u - 2))
                hidden(u, 2, 2, s_up)

            def spread_combine(w):
                m, j = UNITS[WEIGHED[w]]
                if m < SHARED_MB:
                    return
                a, n = PARTS[j]
                pe.wait_ge(s_hid, w)
                c = BLOCKS[m][0] - SHARED
                pe.matmul(ps[:, 7, 0:n], spread_sb[:, c:c + 128], combineT[:, a:a + n],
                          start=True, stop=True).then_inc(s_spread_ps, 1)

            def turn_combine():
                pe.wait_ge(s_combine, 1)
                for t, (a, n) in enumerate(TILES):
                    bank, c = (7, 128 * t) if t < 4 else (6, 0)
                    last = pe.transpose(ps[0:CROWS, bank, c:c + n], combine_split_f[0:n, t, :], ident[0:n, 0:n])
                last.then_inc(s_combine_ps, 1)

            def gather(t):
                return ps[0:TILES[t][1], 4 + t // 2, D * (t % 2):D * (t % 2 + 1)]

            def down_bias():
                pe.wait_ge(s_combineT, 2)
                pe.wait_ge(s_down_hi, 1 + DOWN_SPLITS)
                pe.wait_ge(s_down_lo, 1 + DOWN_SPLITS)
                for t, (a, n) in enumerate(TILES):
                    for i, w in enumerate((down_b_hi, down_b_lo)):
                        pe.matmul(gather(t), combineT[:, a:a + n], w[:, :], start=(i == 0 and t % 2 == 0), stop=False,
                                  skip_group_check=True)

            def down(m, tiles):
                r = rows_of(m)
                upto = LAST_OF[m] if TILES[tiles[-1]][0] >= PARTS[1][0] else FIRST_OF[m]
                pe.wait_ge(s_hid_hi, upto + 1)
                pe.wait_ge(s_hid_lo, upto + 1)
                for t in tiles:
                    a, n = TILES[t]
                    for i, (x, w) in enumerate(((hid_hi, down_hi), (hid_hi, down_lo), (hid_lo, down_hi))):
                        last = pe.matmul(gather(t), x[0:r, m % BLOCK_SLOTS, a:a + n], w[0:r, m, :], start=False,
                                         stop=(m == MB - 1 and i == 2), skip_group_check=True)
                    if m == MB - 1:
                        last.then_inc(s_down, 1)
                if m < MB - 1:
                    last.then_inc(s_block_down, 1)

            embed(0)
            embed(1)
            embed(2)
            embed(3)
            turn(0)
            embed(4)
            turn(1)
            turn(2)
            qk(0)
            kv(0)
            kv(1)
            turn(3)
            turn(4)
            kv(2)
            qk(1)
            outer(0)
            kv(3)
            outer(1)
            kv(4)
            outer(2)
            outer(3)
            attend(0, 0)
            kv(5)
            attend(0, 1)
            outer(4)
            kv(6)
            project(0)
            outer(5)
            project(1)
            kv(7)
            outer(6)
            outer(7)
            attend(1, 0)
            turn(5)
            attend(1, 1)
            turn(6)
            project(2)
            project(3)
            project(4)
            for step in range(STEPS):
                if step == 2:
                    router(0)
                    turn(7)
                if step == 3:
                    turn(8)
                if step == 4:
                    turn(9)
                if step == 5:
                    router(1)
                if step == 6:
                    turn_scores()
                if step == ROUTE_AT:
                    turn_combine()
                    down_bias()
                    pe.wait_ge(s_spread, 1)
                weigh_now = WEIGH_AT[step]
                for w in weigh_now[:1]:
                    spread_combine(w)
                if step < NU:
                    gate(step)
                for w in weigh_now[1:]:
                    spread_combine(w)
                if step < NU:
                    up(step)
                for m, tiles in DOWN_AT.get(step, []):
                    down(m, tiles)

        @block.scalar
        def _(act):
            def root_of(t):
                n = TILES[t % NT][1]
                act.wait_ge(s_var, t + 1)
                act.activation(root[0:n, t, 1:2], root[0:n, t, 0:1], ACT.Sqrt).then_inc(s_root, 1)

            def high_of(t):
                n = TILES[t % NT][1]
                act.wait_ge(s_normed, t + 1)
                if t >= 3:
                    act.wait_ge(s_turned, t - 2)
                act.activation(split_tok[0:n, t % 3, 0:D], normed[0:n, t % 3, :], ACT.Copy).then_inc(s_tok_hi, 1)

            def take_xT(t):
                a, n = TILES[t % NT]
                act.wait_ge(s_turned, t + 1)
                turned = ps[:, turn_bank[t], 0:384].rearrange("p (i t) -> p i t", i=3)
                if t >= NT:
                    last = act.activation(x2T[:, :, a:a + n], turned[:, :, 0:n], ACT.Copy)
                else:
                    first, end = -(-a // TOK), (a + n) // TOK
                    k = first * TOK - a
                    w = (end - first) * TOK
                    if k:
                        act.activation(x1T[:, :, first - 1, TOK - k:TOK], turned[:, :, 0:k], ACT.Copy)
                    for i in range(3):
                        last = act.activation(x1T[:, i, first:end, 0:TOK],
                                              turned[:, i, k:k + w].rearrange("p (m t) -> p m t", t=TOK), ACT.Copy)
                    if k + w < n:
                        last = act.activation(x1T[:, :, end, 0:n - k - w], turned[:, :, k + w:n], ACT.Copy)
                last.then_inc(s_xT, 1)

            def split_moe(m):
                c = m // CHUNK
                w = 4 * rows_of(m)
                act.wait_ge(s_moe_in[c % RAW_SLOTS], 16 * (c // RAW_SLOTS + 1))
                if m >= MOE_SLOTS:
                    act.wait_ge(s_up, 1 + max(u for u in range(NU) if UNITS[u][0] == m - MOE_SLOTS))
                act.activation(moe_hi[:, m % MOE_SLOTS, 0:w], moe_raw[:, c % RAW_SLOTS, 512 * (m % CHUNK):512 * (m % CHUNK) + w],
                               ACT.Copy).then_inc(s_moe_hi, 1)

            def copy_q(j):
                for m in range(2):
                    act.wait_ge(s_q, 2 * j + m + 1)
                    act.wait_ge(s_qk_summed, 4 * j + m + 3)
                    act.activation(qT[:, m, HALF_T * j:HALF_T * (j + 1)].rearrange("p (i t) -> p i t", t=TOK),
                                   ps[0:HALF_D, 6 + m, 0:HALF_I * EVEN].rearrange("p (i t) -> p i t", t=EVEN)[:, :, 0:TOK],
                                   ACT.Copy).then_inc(s_q_copied, 1)

            def copy_kv(p):
                act.wait_ge(s_kv, p + 1)
                if p >= 4:
                    act.wait_ge(s_outer, p - 3)
                act.activation(kv_tok[:, p % 4, :], ps[:, p % 2, 0:2 * D], ACT.Copy).then_inc(s_kv_tok, 1)

            def high_attn(j, m):
                act.wait_ge(s_attn, 2 * j + m + 1)
                act.activation(attn_hi[:, m, HALF_T * j:HALF_T * (j + 1)], ps[0:HALF_D, 6 + m, 0:HALF_T],
                               ACT.Copy).then_inc(s_attn_hi, 1)

            def split_down(i):
                a, n = MB * i // DOWN_SPLITS, MB * (i + 1) // DOWN_SPLITS
                act.activation(down_hi[:, a:n, :], down_raw[:, a:n, :], ACT.Copy).then_inc(s_down_hi, 1)

            for t in range(NT):
                root_of(t)
                if t == 1:
                    act.wait_ge(s_xw, 16)
                    act.activation(xw_hi[:, :, :], xw_raw[:, :, :], ACT.Copy).then_inc(s_xw_hi, 1)
                if t >= 1:
                    high_of(t - 1)
                if t >= 2:
                    take_xT(t - 2)
            high_of(4)
            copy_q(0)
            copy_kv(0)
            copy_kv(1)
            take_xT(3)
            take_xT(4)
            copy_kv(2)
            copy_q(1)
            act.wait_ge(s_small, 16)
            act.activation(w_proj_hi[:, :, :], w_proj[0:HALF_D, :, :], ACT.Copy).then_inc(s_w_proj_hi, 1)
            split_moe(0)
            copy_kv(3)
            split_moe(1)
            copy_kv(4)
            split_moe(2)
            split_moe(3)
            high_attn(0, 0)
            copy_kv(5)
            split_moe(4)
            high_attn(0, 1)
            copy_kv(6)
            split_moe(5)
            act.wait_ge(s_consts, 32)
            act.activation(down_b_hi[:, :], down_b_raw[:, :], ACT.Copy).then_inc(s_down_hi, 1)
            root_of(5)
            copy_kv(7)
            root_of(6)
            high_of(5)
            act.wait_ge(s_down_in, 16)
            split_down(0)
            high_of(6)
            split_down(1)
            high_attn(1, 0)
            take_xT(5)
            high_attn(1, 1)
            take_xT(6)
            split_down(2)
            root_of(7)
            split_down(3)
            root_of(8)
            high_of(7)
            root_of(9)
            high_of(8)

            def sigmoid(u):
                m, j = UNITS[u]
                n, r = PARTS[j][1], rows_of(m)
                act.wait_ge(s_gate, u + 1)
                if u >= S_SLOTS:
                    act.wait_ge(s_gated, u - S_SLOTS + 1)
                act.activation(sig_g[0:r, u % S_SLOTS, 0:n], ps[0:r, u % 2, 0:n], ACT.Sigmoid,
                               bias=col("gate_b")[0:r, m:m + 1]).then_inc(s_sig, 1)

            def scores_of(j):
                a, n = PARTS[j]
                act.wait_ge(s_logits, j + 1)
                act.activation(scoresT[:, a:a + n], ps[0:EXPERTS, 7 if j == 0 else 4, 0:n], ACT.Sigmoid,
                               bias=col("router_b")[0:EXPERTS, :]).then_inc(s_scoresT, 1)

            def high_hid(w):
                m, j = UNITS[WEIGHED[w]]
                (a, n), r = PARTS[j], rows_of(m)
                act.wait_ge(s_hid, w + 1)
                if m >= BLOCK_SLOTS:
                    act.wait_ge(s_block_down, m - BLOCK_SLOTS + 1)
                act.activation(hid_hi[0:r, m % BLOCK_SLOTS, a:a + n], hid[0:r, w % H_SLOTS, 0:n],
                               ACT.Copy).then_inc(s_hid_hi, 1)

            def copy_up(u):
                m, j = UNITS[u]
                n, r, i = PARTS[j][1], rows_of(m), BY_POOL.index(u)
                act.wait_ge(s_up, u + 1)
                if i >= 2:
                    act.wait_ge(s_prod_pool, i - 1)
                act.activation(up_b[0:r, i % 2, 0:n], ps[0:r, 2 + u % 2, 0:n], ACT.Identity,
                               bias=col("up_b")[0:r, m:m + 1]).then_inc(s_up_copied, 1)

            for step in range(STEPS):
                if step < NU:
                    sigmoid(step)
                    if step in BY_POOL:
                        copy_up(step)
                if step == 0:
                    high_of(9)
                if step == 1:
                    scores_of(0)
                    take_xT(7)
                if step == 2:
                    take_xT(8)
                if step == 3:
                    take_xT(9)
                if step == 4:
                    scores_of(1)
                    act.activation(spread_sb[:, :], spread_raw, ACT.Copy).then_inc(s_spread, 1)
                if step >= 1:
                    for w in WEIGH_AT[step - 1]:
                        high_hid(w)
                if step in SPLIT_AT:
                    split_moe(SPLIT_AT[step])
            for w in WEIGH_AT[STEPS - 1]:
                high_hid(w)

        @block.gpsimd
        def _(pool):
            def low(o, x, hi, done):
                pool.tensor_tensor(o, x, hi.bitcast(f32), ALU.subtract).then_inc(done, 1)

            def split_moe(m):
                c = m // CHUNK
                w = 4 * rows_of(m)
                pool.wait_ge(s_moe_hi, m + 1)
                low(moe_lo[:, m % MOE_SLOTS, 0:w], moe_raw[:, c % RAW_SLOTS, 512 * (m % CHUNK):512 * (m % CHUNK) + w],
                    moe_hi[:, m % MOE_SLOTS, 0:w], s_moe_lo)

            def scale_q(j):
                for m in range(2):
                    q = qT[:, m, HALF_T * j:HALF_T * (j + 1)].rearrange("p (i t) -> p i t", t=TOK)
                    pool.wait_ge(s_q_copied, 2 * j + m + 1)
                    pool.wait_ge(s_scale, j + 1)
                    pool.tensor_tensor(q, q, scale_qk[:, j, m, :].unsqueeze(2).broadcast_to([HALF_D, HALF_I, TOK]),
                                       ALU.mult).then_inc(s_qT, 1)

            pool.memset(x1T[:, :, :, TOK:SLOT].bitcast(f32), 0.0)
            pool.memset(scores[:, :, :], 0.0)
            pool.memset(masked[:, :, :], PAD)
            pool.memset(taken8[:, :, :], PAD)
            pool.memset(combine_split[:, :, 2 * EXPERTS:CROWS].bitcast(f32), 1.0).then_inc(s_zero, 1)
            pool.wait_ge(s_xw_hi, 1)
            low(xw_lo[:, :, :], xw_raw[:, :, :], xw_hi[:, :, :], s_xw_lo)
            pool.wait_ge(s_small, 16)
            for t, (a, n) in enumerate(TILES):
                pool.wait_ge(s_h, t + 1)
                pool.tensor_tensor(h2_tok[0:n, t, :], h_tok[0:n, t, :], col("b_proj")[0:n, :], ALU.add).then_inc(s_hb, 1)
            scale_q(0)
            scale_q(1)
            pool.wait_ge(s_w_proj_hi, 1)
            low(w_proj_lo[:, :, :], w_proj[0:HALF_D, :, :], w_proj_hi[:, :, :], s_w_proj_lo)
            for m in range(FIRST_SPLITS):
                split_moe(m)
            pool.wait_ge(s_down_hi, 1)
            low(down_b_lo[:, :], down_b_raw[:, :], down_b_hi[:, :], s_down_lo)
            for i in range(DOWN_SPLITS):
                a, n = MB * i // DOWN_SPLITS, MB * (i + 1) // DOWN_SPLITS
                pool.wait_ge(s_down_hi, i + 2)
                low(down_lo[:, a:n, :], down_raw[:, a:n, :], down_hi[:, a:n, :], s_down_lo)
            for step in range(STEPS):
                if step in BY_POOL:
                    i = BY_POOL.index(step)
                    m, j = UNITS[step]
                    n, r = PARTS[j][1], rows_of(m)
                    p = prod[0:r, step % T_SLOTS, 0:n]
                    pool.wait_ge(s_gated, step + 1)
                    pool.wait_ge(s_up_copied, i + 1)
                    pool.tensor_tensor(p, p, up_b[0:r, i % 2, 0:n], ALU.mult).then_inc(s_prod_pool, 1)
                for w in WEIGH_AT[step]:
                    m, j = UNITS[WEIGHED[w]]
                    (a, n), r = PARTS[j], rows_of(m)
                    pool.wait_ge(s_hid_hi, w + 1)
                    low(hid_lo[0:r, m % BLOCK_SLOTS, a:a + n], hid[0:r, w % H_SLOTS, 0:n],
                        hid_hi[0:r, m % BLOCK_SLOTS, a:a + n], s_hid_lo)
                if step in SPLIT_AT:
                    split_moe(SPLIT_AT[step])

        @block.vector
        def _(dve):
            links = [0]

            def mark(ins):
                links[0] += 1
                ins.then_inc(s_dve, 1)
                return links[0]

            def link(ins):
                dve.wait_ge(s_dve, mark(ins))

            def layer_norm(tiles, first, h, between=None):
                for i in range(len(tiles) + 2):
                    new = first + tiles[i] if i < len(tiles) else None
                    old = first + tiles[i - 1] if 1 <= i <= len(tiles) else None
                    done = first + tiles[i - 2] if i >= 2 else None
                    if new is not None:
                        t, n = new, TILES[new % NT][1]
                        row, s_row = h(t % NT)
                    if old is not None:
                        o, k = old, TILES[old % NT][1]
                        v, r, g, y = (root[0:k, o, c:c + 1] for c in (0, 1, 2, 3))
                        dve.wait_ge(s_root, o + 1)
                        g_at = mark(dve.reciprocal(g, r))
                    if new is not None:
                        dve.wait_ge(*s_row)
                        a = mark(dve.bn_stats(stats[0:n, t % 2, :], row))
                    if old is not None:
                        dve.wait_ge(s_dve, g_at)
                        y_at = mark(dve.scalar_tensor_tensor(out=y, in0=g, scalar=v, in1=g, op0=ALU.mult, op1=ALU.mult))
                    if new is not None:
                        dve.wait_ge(s_dve, a)
                        a = mark(dve.bn_aggr(mean_var[0:n, t, :], stats[0:n, t % 2, :]))
                    if old is not None:
                        dve.wait_ge(s_dve, y_at)
                        c_at = mark(dve.tensor_scalar(root[0:k, o, 4:5], y, -0.5, 1.5, ALU.mult, ALU.add))
                    if new is not None:
                        dve.wait_ge(s_dve, a)
                        dve.tensor_scalar(root[0:n, t, 0:1], mean_var[0:n, t, 1:2], LN_EPS, None, ALU.add).then_inc(s_var, 1)
                    if old is not None:
                        dve.wait_ge(s_dve, c_at)
                        y_at = mark(dve.tensor_tensor(root[0:k, o, 5:6], root[0:k, o, 4:5], g, ALU.mult))
                    if done is not None:
                        k2 = TILES[done % NT][1]
                        dve.wait_ge(s_tok_hi, done + 1)
                        dve.tensor_tensor(split_tok[0:k2, done % 3, D:D + 64], normed[0:k2, done % 3, 128:D],
                                          split_f[0:k2, done % 3, 128:D], ALU.subtract)
                        dve.tensor_tensor(split_tok[0:k2, done % 3, D + 64:2 * D], normed[0:k2, done % 3, 0:128],
                                          split_f[0:k2, done % 3, 0:128], ALU.subtract).then_inc(s_tok_lo, 1)
                    if old is not None:
                        if o >= 3:
                            dve.wait_ge(s_tok_hi, o - 2)
                        dve.wait_ge(s_dve, y_at)
                        hrow = (h_tok if first == 0 else h2_tok)[0:k, o % NT, :]
                        dve.tensor_scalar(normed[0:k, o % 3, :], hrow, mean_var[0:k, o, 0:1], root[0:k, o, 5:6],
                                          ALU.subtract, ALU.mult).then_inc(s_normed, 1)
                    if between:
                        between(i)

            def embedded(t):
                n = TILES[t][1]
                dve.wait_ge(s_embed, t + 1)
                dve.tensor_tensor(h_tok[0:n, t, :], ps[0:n, t % 2, 0:D], base[0:n, t, :], ALU.add).then_inc(s_h, 1)
                return h_tok[0:n, t, :], (s_h, t + 1)

            def attended(t):
                n = TILES[t][1]
                dve.wait_ge(s_proj, t + 1)
                dve.wait_ge(s_hb, t + 1)
                dve.tensor_tensor(h2_tok[0:n, t, :], ps[0:n, proj_bank[t], 0:D], h2_tok[0:n, t, :],
                                  ALU.add).then_inc(s_h2, 1)
                return h2_tok[0:n, t, :], (s_h2, t + 1)

            def qk_sums(j):
                for kind, ready, bank in ((0, s_k, 4), (1, s_q, 6)):
                    for m in range(2):
                        dve.wait_ge(ready, 2 * j + m + 1)
                        dve.tensor_reduce(sums[:, j, kind, m, :],
                                          ps[0:HALF_D, bank + m, 0:HALF_I * EVEN]
                                          .rearrange("p (i t) -> p i t", t=EVEN)[:, :, 0:TOK],
                                          AX.X, ALU.add, apply_absolute_value=True).then_inc(s_qk_summed, 1)
                dve.wait_ge(s_qk_summed, 4 * (j + 1))
                link(dve.tensor_scalar(sums[:, j, :, :, :], sums[:, j, :, :, :], L1_EPS, None, ALU.max))
                link(dve.reciprocal(sums[:, j, :, :, :], sums[:, j, :, :, :]))
                dve.tensor_tensor(scale_qk[:, j, :, :], sums[:, j, 0, :, :], sums[:, j, 1, :, :],
                                  ALU.mult).then_inc(s_scale, 1)

            def mask(p):
                dve.wait_ge(s_outer, p + 1)
                b = 2 + 2 * (p % 2)
                dve.tensor_tensor(kv_blocks[:, 2 * p:2 * p + 2, :], ps[0:HALF_D, b:b + 2, 0:D],
                                  col("blocks")[0:HALF_D, :].unsqueeze(1).broadcast_to([HALF_D, 2, D]),
                                  ALU.mult).then_inc(s_blocks, 1)

            def low_attn(j, m):
                tok = slice(HALF_T * j, HALF_T * (j + 1))
                dve.wait_ge(s_attn_hi, 2 * j + m + 1)
                dve.tensor_tensor(attn_lo[:, m, tok], ps[0:HALF_D, 6 + m, 0:HALF_T],
                                  attn_hi[:, m, tok].bitcast(f32), ALU.subtract).then_inc(s_attn_lo, 1)

            dve.wait_ge(s_first, 16)
            for t, (a, n) in enumerate(TILES):
                dve.scalar_tensor_tensor(out=base[0:n, t, :], in0=col("b")[0:n, :],
                                         scalar=col("token_is_patch")[0:n, t:t + 1], in1=base[0:n, t, :],
                                         op0=ALU.mult, op1=ALU.add).then_inc(s_base, 1)
            dve.wait_ge(s_base, NT)
            layer_norm(range(NT), 0, embedded)
            qk_sums(0)
            qk_sums(1)
            dve.wait_ge(s_small, 16)
            for p in range(4):
                mask(p)
            low_attn(0, 0)
            low_attn(0, 1)
            mask(4)

            def masks_between(i):
                if i == 0:
                    mask(5)
                if i == 1:
                    mask(6)
                    mask(7)

            layer_norm((0, 1), NT, attended, masks_between)
            low_attn(1, 0)
            low_attn(1, 1)
            layer_norm((2, 3, 4), NT, attended)

            def gated(u):
                m, j = UNITS[u]
                n, r = PARTS[j][1], rows_of(m)
                dve.wait_ge(s_gate, u + 1)
                dve.wait_ge(s_sig, u + 1)
                dve.scalar_tensor_tensor(out=prod[0:r, u % T_SLOTS, 0:n], in0=ps[0:r, u % 2, 0:n],
                                         scalar=col("gate_b")[0:r, m:m + 1], in1=sig_g[0:r, u % S_SLOTS, 0:n],
                                         op0=ALU.add, op1=ALU.mult).then_inc(s_gated, 1)

            def times_up(u):
                m, j = UNITS[u]
                n, r = PARTS[j][1], rows_of(m)
                dve.wait_ge(s_up, u + 1)
                dve.wait_ge(s_gated, u + 1)
                dve.scalar_tensor_tensor(out=prod[0:r, u % T_SLOTS, 0:n], in0=ps[0:r, 2 + u % 2, 0:n],
                                         scalar=col("up_b")[0:r, m:m + 1], in1=prod[0:r, u % T_SLOTS, 0:n],
                                         op0=ALU.add, op1=ALU.mult).then_inc(s_prod, 1)

            def weigh(w):
                u = WEIGHED[w]
                m, j = UNITS[u]
                n, r = PARTS[j][1], rows_of(m)
                if u in BY_POOL:
                    dve.wait_ge(s_prod_pool, BY_POOL.index(u) + 1)
                else:
                    dve.wait_ge(s_prod, by_vector(u))
                if w >= H_SLOTS:
                    dve.wait_ge(s_hid_lo, w - H_SLOTS + 1)
                if m >= SHARED_MB:
                    dve.wait_ge(s_spread_ps, w - N_SHARED_UNITS + 1)
                    dve.tensor_tensor(hid[0:r, w % H_SLOTS, 0:n], prod[0:r, u % T_SLOTS, 0:n],
                                      ps[0:r, 7, 0:n], ALU.mult).then_inc(s_hid, 1)
                else:
                    dve.tensor_copy(hid[0:r, w % H_SLOTS, 0:n], prod[0:r, u % T_SLOTS, 0:n]).then_inc(s_hid, 1)

            def take_scores():
                dve.wait_ge(s_zero, 1)
                dve.wait_ge(s_scores_ps, 1)
                full = NT - 1
                n = TILES[full][1]
                dve.tensor_copy(scores[:, 0:full, :],
                                ps[:, 5, 0:EXPERTS * full].rearrange("p (t e) -> p t e", e=EXPERTS)).then_inc(s_scores, 1)
                dve.tensor_copy(scores[0:n, full, :], ps[0:n, 5, EXPERTS * full:EXPERTS * NT]).then_inc(s_scores, 1)
                dve.wait_ge(s_scores, 2)
                link(dve.tensor_tensor(choice[:, :, :], scores[:, :, :],
                                       col("corr").unsqueeze(1).broadcast_to([128, NT, EXPERTS]), ALU.add))

            def group_scores():
                c = choice[:, :, :].rearrange("p t (g e) -> p (t g) e", e=PER_GROUP)
                dve.tensor_tensor(pair_sums[:, :, 0:2], c[:, :, 0:2], c[:, :, 2:4], ALU.add)
                dve.tensor_tensor(pair_sums[:, :, 2:4], c[:, :, 0:4:2], c[:, :, 1:4:2], ALU.add)
                dve.tensor_tensor(pair_sums[:, :, 4:5], c[:, :, 0:1], c[:, :, 3:4], ALU.add)
                link(dve.tensor_tensor(pair_sums[:, :, 5:6], c[:, :, 1:2], c[:, :, 2:3], ALU.add))
                link(dve.tensor_reduce(group_s[:, :, :], pair_sums[:, :, :], AX.X, ALU.max))

            def group_ranks():
                for i, (op, order) in enumerate(((ALU.is_ge, "before"), (ALU.is_gt, "after"))):
                    out4 = beaten[:, i, :, :].rearrange("p t (g o) -> p t g o", o=GROUPS)
                    ins = dve.tensor_tensor(out4, group_s[:, :, :].unsqueeze(2).broadcast_to([128, NT, GROUPS, GROUPS]),
                                            group_s[:, :, :].unsqueeze(3).broadcast_to([128, NT, GROUPS, GROUPS]), op)
                link(ins)
                for i, order in enumerate(("before", "after")):
                    ins = dve.tensor_tensor(beaten[:, i, :, :], beaten[:, i, :, :],
                                            col(order).unsqueeze(1).broadcast_to([128, NT, GROUPS * GROUPS]), ALU.mult)
                link(ins)
                link(dve.tensor_tensor(beaten[:, 0, :, :], beaten[:, 0, :, :], beaten[:, 1, :, :], ALU.add))
                link(dve.tensor_reduce(rank[:, :, :], beaten[:, 0, :, :].rearrange("p t (g o) -> p t g o", o=GROUPS),
                                       AX.X, ALU.add))
                link(dve.tensor_scalar(rank[:, :, :], rank[:, :, :], TOP_GROUPS - 0.5, None, ALU.is_lt))

            def expert_choice():
                g = rank[:, :, :].unsqueeze(3).broadcast_to([128, NT, GROUPS, PER_GROUP])
                link(dve.tensor_tensor(choice[:, :, :].rearrange("p t (g e) -> p t g e", e=PER_GROUP),
                                       choice[:, :, :].rearrange("p t (g e) -> p t g e", e=PER_GROUP), g, ALU.mult))
                link(dve.tensor_scalar(masked[:, :, 0:EXPERTS], choice[:, :, :], 0.0, None, ALU.add))
                for t in range(NT):
                    ins = dve.max(top8[:, t, :], masked[:, t, 0:EXPERTS])
                link(ins)
                link(dve.tensor_copy(taken8[:, :, 0:TOP_K], top8[:, :, 0:TOP_K]))
                for t in range(NT):
                    ins = dve.match_replace(marked[:, t, :], taken8[:, t, :], masked[:, t, :], TAKEN)
                link(ins)

            def combine_weights():
                link(dve.scalar_tensor_tensor(out=weight[:, :, :], in0=marked[:, :, 0:EXPERTS], scalar=TAKEN,
                                              in1=scores[:, :, :], op0=ALU.is_equal, op1=ALU.mult))
                link(dve.tensor_reduce(w_sum[:, 0, :], weight[:, :, :], AX.X, ALU.add))
                link(dve.tensor_scalar(w_sum[:, 1, :], w_sum[:, 0, :], SUM_EPS, None, ALU.add))
                link(dve.reciprocal(w_sum[:, 2, :], w_sum[:, 1, :]))
                link(dve.scalar_tensor_tensor(out=combine[:, :, :], in0=weight[:, :, :], scalar=SCALE,
                                              in1=w_sum[:, 2, :].unsqueeze(2).broadcast_to([128, NT, EXPERTS]),
                                              op0=ALU.mult, op1=ALU.mult))
                link(dve.tensor_copy(combine_split[:, :, 0:EXPERTS], combine[:, :, :]))
                dve.tensor_tensor(combine_split[:, :, EXPERTS:2 * EXPERTS], combine[:, :, :],
                                  combine_split_f[:, :, 0:EXPERTS], ALU.subtract).then_inc(s_combine, 1)

            def take_combine():
                dve.wait_ge(s_combine_ps, 1)
                dve.tensor_copy(combineT[:, 0:512], ps[0:CROWS, 7, 0:512]).then_inc(s_combineT, 1)
                dve.tensor_copy(combineT[:, 512:T], ps[0:CROWS, 6, 0:T - 512]).then_inc(s_combineT, 1)

            for step in range(STEPS):
                if step == 7:
                    take_scores()
                    group_scores()
                if step == 8:
                    group_ranks()
                if step == 9:
                    expert_choice()
                if step == 10:
                    combine_weights()
                if step == ROUTE_AT:
                    take_combine()
                weigh_now = WEIGH_AT[step]
                for w in weigh_now[:1]:
                    weigh(w)
                if step < NU:
                    gated(step)
                for w in weigh_now[1:]:
                    weigh(w)
                if step < NU and step not in BY_POOL:
                    times_up(step)

            for t, (a, n) in enumerate(TILES):
                dve.wait_ge(s_down, min(NT, t // 2 * 2 + 2))
                if t >= 2:
                    dve.wait_ge(s_stored[t % 2], 16 * (t // 2))
                dve.tensor_tensor(out_tok[0:n, t % 2, :], ps[0:n, 4 + t // 2, D * (t % 2):D * (t % 2 + 1)],
                                  h2_tok[0:n, t, :], ALU.add).then_inc(s_out_tok, 1)


def kernel(**inputs):
    import concourse.bacc as _bacc
    from concourse.bass_utils import run_bass_kernel_spmd as _run

    g = {k.replace("L0_", ""): np.asarray(v) for k, v in inputs.items()}
    f = np.float32

    def rows128(a):
        k = -(-a.shape[0] // 128)
        full = np.zeros((k * 128, a.shape[1]), f)
        full[:a.shape[0]] = a
        return full.reshape(k, 128, -1).transpose(1, 0, 2)

    def blocks128(shared, routed):
        return np.concatenate([rows128(shared), rows128(routed)], axis=1)

    x = g["x"].reshape(IMAGES, CHANNELS, GRID, PATCH, GRID, PATCH).transpose(1, 3, 5, 0, 2, 4)
    cols = np.zeros((CHANNELS * PATCH * PATCH, IMAGES, TOK), f)
    cols[:, :, 1:] = x.reshape(-1, IMAGES, GRID * GRID)
    cols = rows128(cols.reshape(-1, T))
    patches = np.concatenate([cols[:, :, a:a + n].reshape(128, -1) for a, n in TILES], axis=1)

    near = np.arange(GRID) * POS_SIDE // GRID
    pos = g["tok_positions"][0][:, near][:, :, near].reshape(D, -1).T
    base = np.concatenate([g["tok_cls_embedding"].reshape(1, D), pos])
    small = np.zeros((128, SMALL_COLS), f)

    def put(name, a, rows=128):
        lo, hi = COLS[name]
        small[:rows, lo:hi] = a

    put("ident", np.eye(128, dtype=f))
    put("token_is_patch", rows128((np.arange(T) % TOK > 0).astype(f)[:, None])[:, :, 0])
    put("b", g["tok_b"][None])
    put("base", rows128(np.tile(base, (IMAGES, 1))).reshape(128, -1))
    patch_w = rows128(g["tok_W"]).reshape(128, -1)
    heads = np.arange(HALF_D) // HEAD
    put("blocks", np.tile((heads[:, None] == heads).astype(f), (1, 2)), HALF_D)
    put("b_proj", g["attn_b_proj"][None])
    put("w_proj", g["attn_w_proj"].T.reshape(2, HALF_D, D).transpose(1, 0, 2).reshape(HALF_D, -1), HALF_D)
    put("router_b", g["ffn_router_b"][:, None], EXPERTS)
    put("corr", g["ffn_corr_bias"][None])
    k = np.arange(GROUPS)
    put("before", (k < k[:, None]).astype(f).reshape(1, -1))
    put("after", (k > k[:, None]).astype(f).reshape(1, -1))
    for name, routed, shared in (("gate_b", "gbg", "sbg"), ("up_b", "gbu", "sbu")):
        put(name, blocks128(g[f"ffn_{shared}"][:, None], g[f"ffn_{routed}"].reshape(-1, 1))[:, :, 0])

    def x_side(w):
        return np.stack([w[:128], np.concatenate([w[128:], w[128:]])], axis=1)

    x_w = x_side(np.concatenate([g["attn_w_qkv"].T, g["ffn_router_w"].T], axis=1))
    gate, up = (x_side(np.concatenate([g[f"ffn_{s}"], g[f"ffn_{r}"].transpose(1, 0, 2).reshape(D, ROUTED)], axis=1))
                for r, s in (("gWg", "sWg"), ("gWu", "sWu")))
    moe_w = np.zeros((128, MB, 512), f)
    for m, (a, n) in enumerate(BLOCKS):
        moe_w[:, m, :4 * n] = np.concatenate([w[:, :, a:a + n].reshape(128, -1) for w in (gate, up)], axis=1)
    moe_w = moe_w.reshape(128, -1)
    down_w = blocks128(g["ffn_sWd"], g["ffn_gWd"].reshape(ROUTED, D))
    down_b = np.concatenate([g["ffn_gbd"], g["ffn_gbd"], g["ffn_sbd"][None]])
    of = (np.arange(ROUTED) // INNER == np.arange(EXPERTS)[:, None]).astype(f)
    spread = np.concatenate([of, of, np.zeros((1, ROUTED), f)])

    nc = _bacc.Bacc("TRN2", target_bir_lowering=False, num_devices=1)
    arrays, args = {}, []
    for name, a in (("patches", patches), ("patch_w", patch_w), ("small", small), ("x_w", x_w), ("moe_w", moe_w), ("down_w", down_w),
                    ("down_b", down_b), ("spread", spread)):
        a = np.ascontiguousarray(a)
        arrays[f"in_{name}"] = a
        args.append(nc.dram_tensor(f"in_{name}", a.shape, mybir.dt.from_np(a.dtype), kind="ExternalInput").ap())
    args.append(nc.dram_tensor("out_tokens", (T, D), mybir.dt.float32, kind="ExternalOutput").ap())
    tower(nc, *args)
    r = _run(nc, [arrays], core_ids=[0])
    return r.results[0]["out_tokens"].reshape(IMAGES, TOK, D)
```

```python
import numpy as np
import concourse.bass as bass
from concourse import mybir
from contextlib import ExitStack

IMAGES, CHANNELS, SIDE, PATCH = 16, 3, 96, 16
GRID = SIDE // PATCH
POS_SIDE = 14
D = 192
TOK = GRID * GRID + 1
T = IMAGES * TOK
TILES = [(t, min(128, T - t)) for t in range(0, T, 128)]
NT = len(TILES)
PATCH_K = CHANNELS * PATCH * PATCH // 128
HEAD, HALF_D = 16, D // 2
SLOT = 64
EVEN = TOK + 1
HALF_T = T // 2
HALF_I = IMAGES // 2
PAIRS = IMAGES // 2
EXPERTS, GROUPS, INNER = 16, 4, 96
PER_GROUP = EXPERTS // GROUPS
TOP_GROUPS, TOP_K, SCALE = 2, 4, 2.5
ROUTED, SHARED = EXPERTS * INNER, 2 * INNER
HID = ROUTED + SHARED
BLOCKS = [(a, min(128, SHARED - a)) for a in range(0, SHARED, 128)]
SHARED_MB = len(BLOCKS)
BLOCKS += [(a, 128) for a in range(SHARED, HID, 128)]
MB = len(BLOCKS)
PARTS = [(0, 2 * 128), (2 * 128, T - 2 * 128)]
PART_MAX = max(n for _, n in PARTS)
EARLY = 5
UNITS = [(m, j) for j in range(2) for m in range(EARLY)] + [(m, j) for m in range(EARLY, MB) for j in range(2)]
NU = len(UNITS)
LN_EPS, L1_EPS, SUM_EPS = 1e-5, 1e-12, 1e-20
XW = 3 * D + EXPERTS
XW_SPLITS = [(0, 2 * D), (2 * D, D + EXPERTS)]
CROWS = 2 * EXPERTS + 1
PAD, TAKEN = -3e38, 3e38


def rows_of(m):
    return BLOCKS[m][1]


_at = 0
COLS = {}
for _name, _n in (("token_is_patch", NT), ("b", D), ("base", NT * D), ("ident", 128), ("blocks", D), ("b_proj", D),
                  ("w_proj", 2 * D), ("router_b", 1), ("corr", EXPERTS), ("before", GROUPS * GROUPS),
                  ("after", GROUPS * GROUPS), ("gate_b", MB), ("up_b", MB)):
    COLS[_name] = (_at, _at + _n)
    _at += _n
BASE_COLS = COLS["base"][0] + 2 * D
FIRST_COLS = COLS["blocks"][0]
SMALL_COLS = _at

CHUNK = 2
CHUNKS = MB // CHUNK
RAW_SLOTS = 3
ROUTE_AT, LAG = 13, 2
WEIGHED = [u for u in range(NU) if UNITS[u][0] < SHARED_MB]
WEIGHED += sorted((u for u in range(NU) if UNITS[u][0] >= SHARED_MB), key=lambda u: UNITS[u])
N_SHARED_UNITS = 2 * SHARED_MB
FIRST_OF, LAST_OF = ([WEIGHED.index(UNITS.index((m, j))) for m in range(MB)] for j in range(2))
BY_POOL = list(range(6, 13))
SCORES_AT, CHOOSE_AT, SUMS_AT, WEIGHTS_AT = 7, 9, 10, 10
FIRST_SPLITS = 6
SPLIT_AHEAD = 4
SPLIT_AT = {3: 6, 5: 7}
SPLIT_AT.update({2 * m - SPLIT_AHEAD: m for m in range(8, MB)})
DOWN_CHUNKS = [0, 3, 7, 10]
DOWN_SPLIT_AT = {14: 2, 16: 3}


def by_vector(u):
    return u + 1 - sum(p <= u for p in BY_POOL)


def steps():
    at, step, w = [], 0, 0
    while w < NU:
        now = []
        while w < NU and len(now) < 2 and WEIGHED[w] <= step - LAG and (w < N_SHARED_UNITS or step >= ROUTE_AT):
            now.append(w)
            w += 1
        at.append(now)
        step += 1
    when = {w: s for s, now in enumerate(at) for w in now}
    down = {}
    for m in range(MB):
        for tiles, w in (((0, 1), FIRST_OF[m]), ((2, 3, 4), LAST_OF[m])) if m == MB - 1 else ((range(NT), LAST_OF[m]),):
            down.setdefault(max(when[w] + 2 + (m == MB - 3), ROUTE_AT + m), []).append((m, list(tiles)))
    return at, down


WEIGH_AT, DOWN_AT = steps()
STEPS = max(DOWN_AT) + 1
WEIGH_AT += [[]] * (STEPS - len(WEIGH_AT))
WARMING = 7
MOE_SLOTS = 8
T_SLOTS, S_SLOTS, H_SLOTS, BLOCK_SLOTS, UP_SLOTS = 12, 2, 3, 3, 3


def tower(nc, patches, patch_w_in, small, x_w, moe_w, down_w, down_b, spread, out):
    dt = mybir.dt
    f32, f32r = dt.float32, dt.float32r
    ALU = mybir.AluOpType
    ACT = mybir.ActivationFunctionType
    AX = mybir.AxisListType

    with ExitStack() as ctx:
        def sb(name, shape, t=f32):
            return ctx.enter_context(nc.sbuf_tensor(name, shape, t))

        def sem(name):
            return ctx.enter_context(nc.semaphore(name))

        patch_sb = sb("patch_sb", [128, PATCH_K * (T + D)])
        small_sb = sb("small_sb", [128, SMALL_COLS])
        xw_raw = sb("xw_raw", [128, 2, XW])
        moe_raw = sb("moe_raw", [128, RAW_SLOTS, CHUNK * 512])
        down_raw = patch_sb[:, 0:MB * D].rearrange("p (m d) -> p m d", d=D)
        down_b_raw = sb("down_b_raw", [CROWS, D])
        spread_raw = patch_sb[0:CROWS, MB * D:MB * D + ROUTED]
        xw_hi = sb("xw_hi", [128, 2, XW], f32r)
        xw_lo = sb("xw_lo", [128, 2, XW], f32r)
        moe_hi = sb("moe_hi", [128, MOE_SLOTS, 512], f32r)
        moe_lo = sb("moe_lo", [128, MOE_SLOTS, 512], f32r)
        down_hi = sb("down_hi", [128, MB, D], f32r)
        down_lo = sb("down_lo", [128, MB, D], f32r)
        down_b_hi = sb("down_b_hi", [CROWS, D], f32r)
        down_b_lo = sb("down_b_lo", [CROWS, D], f32r)
        spread_sb = sb("spread_sb", [CROWS, ROUTED], f32r)
        h_tok = sb("h_tok", [128, NT, D])
        h2_tok = sb("h2_tok", [128, NT, D])
        half_power = sb("half_power", [128, 1])
        stats = sb("stats", [128, 2, 6])
        mean_var = sb("mean_var", [128, 2 * NT, 2])
        root = sb("root", [128, 2 * NT, 5])
        normed = sb("normed", [128, 3, D])
        split_tok = sb("split_tok", [128, 3, 2 * D], f32r)
        x1T = sb("x1T", [128, 3, IMAGES, SLOT], f32r)
        x2T = x1T[:, :, :, :].rearrange("p i m t -> p i (m t)")[:, :, 0:T]
        sums = sb("sums", [HALF_D, 2, 2, 2, HALF_I])
        scale_qk = sb("scale_qk", [HALF_D, 2, 2, HALF_I])
        kv_tok = sb("kv_tok", [128, 4, 2 * D])
        wide = sb("wide", [128, max(IMAGES * D + 2 * T, T_SLOTS * PART_MAX)])
        kv_blocks = wide[0:HALF_D, 0:IMAGES * D].rearrange("p (i d) -> p i d", d=D)
        qT = wide[0:HALF_D, IMAGES * D:IMAGES * D + 2 * T].rearrange("p (m t) -> p m t", t=T)
        idle = sb("idle", [128, 128], dt.bfloat16)
        prod = wide[:, 0:T_SLOTS * PART_MAX].rearrange("p (s t) -> p s t", t=PART_MAX)
        attn_hi = sb("attn_hi", [HALF_D, 2, T], f32r)
        attn_lo = sb("attn_lo", [HALF_D, 2, T], f32r)
        w_proj_hi = sb("w_proj_hi", [HALF_D, 2, D], f32r)
        w_proj_lo = sb("w_proj_lo", [HALF_D, 2, D], f32r)
        scoresT = sb("scoresT", [EXPERTS, T])
        scores = sb("scores", [128, NT, EXPERTS])
        choice = sb("choice", [128, NT, EXPERTS])
        pair_sums = sb("pair_sums", [128, NT * GROUPS, 6])
        group_s = sb("group_s", [128, NT, GROUPS])
        beaten = sb("beaten", [128, 2, NT, GROUPS * GROUPS])
        rank = sb("rank", [128, NT, GROUPS])
        masked = sb("masked", [128, NT, EXPERTS + TOP_K])
        top8 = sb("top8", [128, NT, 8])
        taken8 = sb("taken8", [128, NT, 8])
        marked = sb("marked", [128, NT, EXPERTS + TOP_K])
        weight = sb("weight", [128, NT, EXPERTS])
        w_sum = sb("w_sum", [128, 3, NT])
        combine = sb("combine", [128, NT, EXPERTS])
        combine_split = sb("combine_split", [128, NT, CROWS], f32r)
        combineT = sb("combineT", [CROWS, T], f32r)
        sig_g = sb("sig_g", [128, S_SLOTS, PART_MAX])
        up_b = sb("up_b", [128, UP_SLOTS, PART_MAX])
        hid = xw_raw[:, :, :].rearrange("p i n -> p (i n)")[:, 0:H_SLOTS * PART_MAX]
        hid = hid.rearrange("p (s t) -> p s t", t=PART_MAX)
        hid_hi = sb("hid_hi", [128, BLOCK_SLOTS, T], f32r)
        hid_lo = sb("hid_lo", [128, BLOCK_SLOTS, T], f32r)

        ps = ctx.enter_context(nc.psum_tensor("ps", [128, 8, 512], f32))

        def col(name):
            a, b = COLS[name]
            return small_sb[:, a:b]

        ident = col("ident")
        base = col("base").rearrange("p (t d) -> p t d", d=D)
        patch_w = patch_sb[:, PATCH_K * T:PATCH_K * (T + D)].rearrange("p (k d) -> p k d", d=D)
        w_proj = col("w_proj").rearrange("p (m d) -> p m d", d=D)
        split_f = split_tok[:, :, :].bitcast(f32)
        combine_split_f = combine_split[:, :, :].bitcast(f32)

        s_patch_0 = [sem(f"s_patch_0_{i}") for i in range(2)]
        s_patch = [sem(f"s_patch{t}") for t in range(NT)]
        s_patch_w = [sem(f"s_patch_w{i}") for i in range(2)]
        s_first, s_second, s_small = sem("s_first"), sem("s_second"), sem("s_small")
        s_xw, s_consts = sem("s_xw"), sem("s_consts")
        s_idle = sem("s_idle")
        s_moe_in = [sem(f"s_moe_in{i}") for i in range(RAW_SLOTS)]
        s_down_in = sem("s_down_in")
        s_moe_hi, s_moe_lo = sem("s_moe_hi"), sem("s_moe_lo")
        s_xw_hi, s_xw_lo, s_xw_lo_1 = sem("s_xw_hi"), sem("s_xw_lo"), sem("s_xw_lo_1")
        s_down_hi, s_down_lo = sem("s_down_hi"), sem("s_down_lo")
        s_spread = sem("s_spread")
        s_zero = sem("s_zero")
        s_base = sem("s_base")
        s_embed = sem("s_embed")
        s_var = sem("s_var")
        s_root = sem("s_root")
        s_normed = sem("s_normed")
        s_tok_hi, s_tok_lo = sem("s_tok_hi"), sem("s_tok_lo")
        s_turned = sem("s_turned")
        s_xT = sem("s_xT")
        s_k, s_q = sem("s_k"), sem("s_q")
        s_qk_summed, s_q_copied, s_scale, s_qT = sem("s_qk_summed"), sem("s_q_copied"), sem("s_scale"), sem("s_qT")
        s_w_proj_hi, s_w_proj_lo = sem("s_w_proj_hi"), sem("s_w_proj_lo")
        s_kv, s_kv_tok = sem("s_kv"), sem("s_kv_tok")
        s_outer, s_blocks = sem("s_outer"), sem("s_blocks")
        s_attn, s_attn_hi, s_attn_lo = sem("s_attn"), sem("s_attn_hi"), sem("s_attn_lo")
        s_hb = sem("s_hb")
        s_h = sem("s_h")
        s_proj = sem("s_proj")
        s_h2 = sem("s_h2")
        s_logits, s_scoresT, s_scores_ps, s_scores = sem("s_logits"), sem("s_scoresT"), sem("s_scores_ps"), sem("s_scores")
        s_beaten, s_masked = sem("s_beaten"), sem("s_masked")
        s_combine, s_combine_ps, s_combineT = sem("s_combine"), sem("s_combine_ps"), sem("s_combineT")
        s_gate, s_up, s_spread_ps = sem("s_gate"), sem("s_up"), sem("s_spread_ps")
        s_sig, s_gated, s_prod, s_hid = sem("s_sig"), sem("s_gated"), sem("s_prod"), sem("s_hid")
        s_hid_hi, s_hid_lo = sem("s_hid_hi"), sem("s_hid_lo")
        s_up_copied, s_prod_pool = sem("s_up_copied"), sem("s_prod_pool")
        s_block_down = sem("s_block_down")
        s_down, s_out_tok = sem("s_down"), sem("s_out_tok")
        s_stored = sem("s_stored")
        s_dve, s_pool = sem("s_dve"), sem("s_pool")

        block = ctx.enter_context(nc.Block())

        @block.sync
        def _(sp):
            def load_small(a, b, sem_):
                sp.dma_start(small_sb[:, a:b], small[:, a:b]).then_inc(sem_, 16)

            def load_patches(t):
                a, n = TILES[t]
                sp.dma_start(patch_sb[:, PATCH_K * a:PATCH_K * (a + n)],
                             patches[:, PATCH_K * a:PATCH_K * (a + n)]).then_inc(s_patch[t], 16)

            def load_first_patches(i):
                n = PATCH_K // 2 * TILES[0][1]
                sp.dma_start(patch_sb[:, n * i:n * (i + 1)], patches[:, n * i:n * (i + 1)]).then_inc(s_patch_0[i], 16)

            half_w = PATCH_K * D // 2

            def load_patch_w(i):
                sp.dma_start(patch_sb[:, PATCH_K * T + half_w * i:PATCH_K * T + half_w * (i + 1)],
                             patch_w_in[:, half_w * i:half_w * (i + 1)]).then_inc(s_patch_w[i], 16)

            load_patch_w(0)
            load_first_patches(0)
            load_patch_w(1)
            load_first_patches(1)
            load_small(0, BASE_COLS, s_first)
            load_patches(1)
            load_patches(2)
            load_small(BASE_COLS, FIRST_COLS, s_second)
            load_patches(3)
            sp.dma_start(xw_raw[:, :, :], x_w).then_inc(s_xw, 16)
            load_patches(4)
            load_small(FIRST_COLS, SMALL_COLS, s_small)
            for c in range(CHUNKS):
                if c >= RAW_SLOTS:
                    sp.wait_ge(s_moe_hi, CHUNK * (c - RAW_SLOTS + 1))
                    sp.wait_ge(s_moe_lo, CHUNK * (c - RAW_SLOTS + 1))
                a = 512 * CHUNK * c
                sp.dma_start(moe_raw[:, c % RAW_SLOTS, :], moe_w[:, a:a + 512 * CHUNK]).then_inc(s_moe_in[c % RAW_SLOTS], 16)
                if c == RAW_SLOTS - 1:
                    sp.dma_start(down_b_raw[:, :], down_b).then_inc(s_consts, 16)
                    sp.wait_ge(s_embed, NT)
                    sp.dma_start(spread_raw, spread).then_inc(s_consts, 16)
                    sp.dma_start(down_raw, down_w).then_inc(s_down_in, 16)
            for i, t in enumerate(range(0, NT, 2)):
                a, n = TILES[t]
                tiles = min(2, NT - t)
                sp.wait_ge(s_out_tok, i + 1)
                sp.dma_start(out[a:a + tiles * n, :].rearrange("(t p) d -> p t d", p=n),
                             h2_tok[0:n, t:t + tiles, :]).then_inc(s_stored, 16)
            sp.wait_ge(s_stored, 16 * ((NT + 1) // 2))

        turn_bank = [2, 3, 2, 3, 2] + [2, 3, 4, 5, 6]
        proj_bank = [0, 1, 0, 1, 4]

        @block.tensor
        def _(pe):
            def product(o, hi, lo, x, tokens_are_weights=False):
                terms = ((hi[0], 0), (lo[0], 0), (hi[0], 2), (hi[1], 1), (lo[1], 1))
                for i, (w, part) in enumerate(terms):
                    a, b = (x(part), w) if tokens_are_weights else (w, x(part))
                    last = pe.matmul(o, a, b, start=(i == 0), stop=(i == len(terms) - 1))
                return last

            def keep_warm(products, bank):
                for i in range(products):
                    pe.matmul(ps[:, bank, :], idle[:, :], idle[:, :].unsqueeze(1).broadcast_to([128, 4, 128]),
                              start=True, stop=True)

            def x_weights(a, b):
                return [xw_hi[:, i, a:b] for i in range(2)], [xw_lo[:, i, a:b] for i in range(2)]

            def embed(t):
                a, n = TILES[t]
                if t >= 1:
                    pe.wait_ge(s_patch[t], 16)
                if t >= 2:
                    pe.wait_ge(s_h, t - 1)
                tile = patch_sb[:, PATCH_K * a:PATCH_K * (a + n)].rearrange("p (k t) -> p k t", k=PATCH_K)
                for k in range(PATCH_K):
                    if t == 0 and k % (PATCH_K // 2) == 0:
                        pe.wait_ge(s_patch_w[k // (PATCH_K // 2)], 16)
                        pe.wait_ge(s_patch_0[k // (PATCH_K // 2)], 16)
                    last = pe.matmul(ps[0:n, t % 2, 0:D], tile[:, k, :], patch_w[:, k, :],
                                     start=(k == 0), stop=(k == PATCH_K - 1))
                last.then_inc(s_embed, 1)

            def turn(t):
                a, n = TILES[t % NT]
                if t == 0:
                    pe.wait_ge(s_second, 16)
                pe.wait_ge(s_tok_hi, t + 1)
                pe.wait_ge(s_tok_lo, t + 1)
                if t == NT + 2:
                    pe.wait_ge(s_h2, NT)
                if 2 <= t < NT:
                    pe.wait_ge(s_xT, t - 1)
                for i in range(3):
                    last = pe.transpose(ps[:, turn_bank[t], 128 * i:128 * i + n],
                                        split_f[0:n, t % 3, 128 * i:128 * i + 128], ident[0:n, 0:n])
                last.then_inc(s_turned, 1)

            def qk(j):
                pe.wait_ge(s_xT, 3 if j == 0 else NT)
                if j == 0:
                    pe.wait_ge(s_xw_hi, 1)
                    pe.wait_ge(s_xw_lo, 1)
                    pe.wait_ge(s_xw_lo_1, 1)
                    pe.wait_ge(s_zero, 1)
                else:
                    pe.wait_ge(s_qk_summed, 4)
                    pe.wait_ge(s_q_copied, 2)
                im = slice(HALF_I * j, HALF_I * (j + 1))
                for kind, done, bank in ((1, s_k, 4), (0, s_q, 6)):
                    for m in range(2):
                        c = D * kind + HALF_D * m
                        product(ps[0:HALF_D, bank + m, 0:HALF_I * EVEN], *x_weights(c, c + HALF_D),
                                lambda i: x1T[:, i, im, 0:EVEN]).then_inc(done, 1)

            def kv(p):
                if p == 0:
                    pe.wait_ge(s_xw_hi, 2)
                    pe.wait_ge(s_xw_lo, 3)
                    pe.wait_ge(s_h, NT)
                if p == 4:
                    pe.wait_ge(s_xT, NT)
                if p >= 2:
                    pe.wait_ge(s_kv_tok, p - 1)
                product(ps[:, p % 2, 0:2 * D], *x_weights(D, 3 * D),
                        lambda i: x1T[:, i, 2 * p:2 * p + 2, :].rearrange("p m t -> p (m t)"), True).then_inc(s_kv, 1)

            def outer(p):
                pe.wait_ge(s_kv_tok, p + 1)
                if p >= 2:
                    pe.wait_ge(s_blocks, p - 1)
                if p == 0:
                    pe.wait_ge(s_xT, NT)
                if p == 1:
                    pe.wait_ge(s_qk_summed, 6)
                for m in range(2):
                    for i in range(2):
                        r = slice(64 * i, 64 * i + TOK)
                        last = pe.matmul(ps[0:HALF_D, 2 + 2 * (p % 2) + i, HALF_D * m:HALF_D * (m + 1)],
                                         kv_tok[r, p % 4, HALF_D * m:HALF_D * (m + 1)],
                                         kv_tok[r, p % 4, D + HALF_D * m:D + HALF_D * (m + 1)],
                                         start=True, stop=True)
                last.then_inc(s_outer, 1)

            def attend(j, m):
                pe.wait_ge(s_qT, 2 * (j + 1))
                pe.wait_ge(s_blocks, PAIRS // 2 * (j + 1))
                if j == 0:
                    pe.wait_ge(s_qk_summed, 8)
                    pe.wait_ge(s_q_copied, 4)
                else:
                    pe.wait_ge(s_attn_lo, m + 1)
                for i in range(HALF_I):
                    im = HALF_I * j + i
                    last = pe.matmul(ps[0:HALF_D, 6 + m, TOK * i:TOK * (i + 1)],
                                     kv_blocks[:, im, HALF_D * m:HALF_D * (m + 1)],
                                     qT[:, m, TOK * im:TOK * (im + 1)], start=True, stop=True)
                last.then_inc(s_attn, 1)

            def project(t):
                a, n = TILES[t]
                half = 1 if a + n <= HALF_T else 2
                pe.wait_ge(s_attn_hi, 2 * half)
                pe.wait_ge(s_attn_lo, 2 * half)
                if t == 0:
                    pe.wait_ge(s_w_proj_hi, 1)
                    pe.wait_ge(s_w_proj_lo, 1)
                    pe.wait_ge(s_kv_tok, PAIRS)
                if t >= 2:
                    pe.wait_ge(s_h2, min(2, t - 1))
                terms = [(x, w, m) for x, w in ((attn_hi, w_proj_hi), (attn_hi, w_proj_lo), (attn_lo, w_proj_hi))
                         for m in range(2)]
                for i, (x, w, m) in enumerate(terms):
                    last = pe.matmul(ps[0:n, proj_bank[t], 0:D], x[:, m, a:a + n], w[:, m, :],
                                     start=(i == 0), stop=(i == len(terms) - 1))
                last.then_inc(s_proj, 1)

            def router(j):
                a, n = PARTS[j]
                pe.wait_ge(s_xT, NT + 2 if j == 0 else 2 * NT)
                pe.wait_ge(s_attn_lo, 4)
                product(ps[0:EXPERTS, 7 if j == 0 else 4, 0:n], *x_weights(3 * D, XW),
                        lambda i: x2T[:, i, a:a + n]).then_inc(s_logits, 1)

            def turn_scores():
                pe.wait_ge(s_scoresT, 2)
                for t, (a, n) in enumerate(TILES):
                    last = pe.transpose(ps[0:n, 5, EXPERTS * t:EXPERTS * (t + 1)], scoresT[:, a:a + n],
                                        ident[0:EXPERTS, 0:EXPERTS])
                last.then_inc(s_scores_ps, 1)

            def hidden(u, at, bank, done):
                m, j = UNITS[u]
                a, n = PARTS[j]
                r = rows_of(m)
                at *= r
                hi, lo = moe_hi[:, m % MOE_SLOTS, :], moe_lo[:, m % MOE_SLOTS, :]
                product(ps[0:r, bank + u % 2, 0:n],
                        [hi[:, at:at + r], hi[:, at + r:at + 2 * r]], [lo[:, at:at + r], lo[:, at + r:at + 2 * r]],
                        lambda i: x2T[:, i, a:a + n]).then_inc(done, 1)

            def gate(u):
                m, j = UNITS[u]
                pe.wait_ge(s_moe_hi, m + 1)
                pe.wait_ge(s_moe_lo, m + 1)
                if u == 0:
                    pe.wait_ge(s_xT, NT + 2)
                if u < 2:
                    pe.wait_ge(s_h2, u + 3)
                if j == 1:
                    pe.wait_ge(s_xT, 2 * NT)
                if u >= 2:
                    pe.wait_ge(s_gated, u - 1)
                hidden(u, 0, 0, s_gate)

            def up(u):
                if u >= 2:
                    if u - 2 in BY_POOL:
                        pe.wait_ge(s_up_copied, BY_POOL.index(u - 2) + 1)
                    else:
                        pe.wait_ge(s_prod, by_vector(u - 2))
                hidden(u, 2, 2, s_up)

            def spread_combine(w):
                m, j = UNITS[WEIGHED[w]]
                if m < SHARED_MB:
                    return
                a, n = PARTS[j]
                pe.wait_ge(s_hid, w)
                c = BLOCKS[m][0] - SHARED
                pe.matmul(ps[:, 7, 0:n], spread_sb[:, c:c + 128], combineT[:, a:a + n],
                          start=True, stop=True).then_inc(s_spread_ps, 1)

            def turn_combine():
                pe.wait_ge(s_combine, 1)
                for t, (a, n) in enumerate(TILES):
                    bank, c = (7, 128 * t) if t < 4 else (6, 0)
                    last = pe.transpose(ps[0:CROWS, bank, c:c + n], combine_split_f[0:n, t, :], ident[0:n, 0:n])
                last.then_inc(s_combine_ps, 1)

            def gather(t):
                return ps[0:TILES[t][1], 4 + t // 2, D * (t % 2):D * (t % 2 + 1)]

            def down_bias():
                pe.wait_ge(s_down_hi, 1)
                pe.wait_ge(s_down_lo, 1)
                for t, (a, n) in enumerate(TILES):
                    for i, w in enumerate((down_b_hi, down_b_lo)):
                        pe.matmul(gather(t), combineT[:, a:a + n], w[:, :], start=(i == 0 and t % 2 == 0), stop=False,
                                  skip_group_check=True)

            def down(m, tiles):
                r = rows_of(m)
                upto = LAST_OF[m] if TILES[tiles[-1]][0] >= PARTS[1][0] else FIRST_OF[m]
                if m in DOWN_CHUNKS:
                    pe.wait_ge(s_down_hi, 2 + DOWN_CHUNKS.index(m))
                    pe.wait_ge(s_down_lo, 2 + DOWN_CHUNKS.index(m))
                pe.wait_ge(s_hid_hi, upto + 1)
                pe.wait_ge(s_hid_lo, upto + 1)
                for t in tiles:
                    a, n = TILES[t]
                    for i, (x, w) in enumerate(((hid_hi, down_hi), (hid_hi, down_lo), (hid_lo, down_hi))):
                        last = pe.matmul(gather(t), x[0:r, m % BLOCK_SLOTS, a:a + n], w[0:r, m, :], start=False,
                                         stop=(m == MB - 1 and i == 2), skip_group_check=True)
                    if m == MB - 1:
                        last.then_inc(s_down, 1)
                if m < MB - 1:
                    last.then_inc(s_block_down, 1)

            pe.wait_ge(s_idle, 1)
            keep_warm(WARMING, 7)
            embed(0)
            embed(1)
            embed(2)
            embed(3)
            turn(0)
            embed(4)
            turn(1)
            turn(2)
            qk(0)
            kv(0)
            turn(3)
            kv(1)
            turn(4)
            kv(2)
            outer(0)
            qk(1)
            outer(1)
            kv(3)
            outer(2)
            outer(3)
            kv(4)
            attend(0, 0)
            kv(5)
            outer(4)
            attend(0, 1)
            kv(6)
            kv(7)
            outer(5)
            project(0)
            outer(6)
            outer(7)
            project(1)
            pe.wait_ge(s_attn_lo, 1)
            keep_warm(2, 6)
            attend(1, 0)
            attend(1, 1)
            keep_warm(2, 5)
            turn(5)
            keep_warm(3, 5)
            project(2)
            turn(6)
            project(3)
            project(4)
            for step in range(STEPS):
                if step == 2:
                    router(0)
                    turn(7)
                if step == 3:
                    turn(8)
                if step == 4:
                    turn(9)
                if step == 5:
                    router(1)
                if step == 6:
                    turn_scores()
                weigh_now = WEIGH_AT[step]
                if step < NU:
                    gate(step)
                if step == ROUTE_AT:
                    up(step)
                    pe.wait_ge(s_combineT, 2)
                    pe.wait_ge(s_spread, 1)
                for w in weigh_now[:1]:
                    spread_combine(w)
                if step == ROUTE_AT:
                    down_bias()
                elif step < NU:
                    up(step)
                if step == ROUTE_AT - 1:
                    turn_combine()
                for w in weigh_now[1:]:
                    spread_combine(w)
                for m, tiles in DOWN_AT.get(step, []):
                    down(m, tiles)

        @block.scalar
        def _(act):
            def high_of(t):
                n = TILES[t % NT][1]
                act.wait_ge(s_normed, t + 1)
                if t >= 3:
                    act.wait_ge(s_turned, t - 2)
                act.activation(split_tok[0:n, t % 3, 0:D], normed[0:n, t % 3, :], ACT.Copy).then_inc(s_tok_hi, 1)

            def take_xT(t):
                a, n = TILES[t % NT]
                act.wait_ge(s_turned, t + 1)
                turned = ps[:, turn_bank[t], 0:384].rearrange("p (i t) -> p i t", i=3)
                if t >= NT:
                    last = act.activation(x2T[:, :, a:a + n], turned[:, :, 0:n], ACT.Copy)
                else:
                    first, end = -(-a // TOK), (a + n) // TOK
                    k = first * TOK - a
                    w = (end - first) * TOK
                    if k:
                        act.activation(x1T[:, :, first - 1, TOK - k:TOK], turned[:, :, 0:k], ACT.Copy)
                    for i in range(3):
                        last = act.activation(x1T[:, i, first:end, 0:TOK],
                                              turned[:, i, k:k + w].rearrange("p (m t) -> p m t", t=TOK), ACT.Copy)
                    if k + w < n:
                        last = act.activation(x1T[:, :, end, 0:n - k - w], turned[:, :, k + w:n], ACT.Copy)
                last.then_inc(s_xT, 1)

            def split_moe(m):
                c = m // CHUNK
                w = 4 * rows_of(m)
                act.wait_ge(s_moe_in[c % RAW_SLOTS], 16 * (c // RAW_SLOTS + 1))
                if m >= MOE_SLOTS:
                    act.wait_ge(s_up, 1 + max(u for u in range(NU) if UNITS[u][0] == m - MOE_SLOTS))
                a = 512 * (m % CHUNK)
                act.activation(moe_hi[:, m % MOE_SLOTS, 0:w], moe_raw[:, c % RAW_SLOTS, a:a + w], ACT.Copy).then_inc(s_moe_hi, 1)

            def copy_q(j):
                for m in range(2):
                    act.wait_ge(s_q, 2 * j + m + 1)
                    act.wait_ge(s_qk_summed, 4 * j + m + 3)
                    act.activation(qT[:, m, HALF_T * j:HALF_T * (j + 1)].rearrange("p (i t) -> p i t", t=TOK),
                                   ps[0:HALF_D, 6 + m, 0:HALF_I * EVEN].rearrange("p (i t) -> p i t", t=EVEN)[:, :, 0:TOK],
                                   ACT.Copy).then_inc(s_q_copied, 1)

            def copy_kv(p):
                act.wait_ge(s_kv, p + 1)
                if p >= 4:
                    act.wait_ge(s_outer, p - 3)
                act.activation(kv_tok[:, p % 4, :], ps[:, p % 2, 0:2 * D], ACT.Copy).then_inc(s_kv_tok, 1)

            def high_attn(j, m):
                act.wait_ge(s_attn, 2 * j + m + 1)
                act.activation(attn_hi[:, m, HALF_T * j:HALF_T * (j + 1)], ps[0:HALF_D, 6 + m, 0:HALF_T],
                               ACT.Copy).then_inc(s_attn_hi, 1)

            def sigmoid(u):
                m, j = UNITS[u]
                n, r = PARTS[j][1], rows_of(m)
                act.wait_ge(s_gate, u + 1)
                if u >= S_SLOTS:
                    act.wait_ge(s_gated, u - S_SLOTS + 1)
                act.activation(sig_g[0:r, u % S_SLOTS, 0:n], ps[0:r, u % 2, 0:n], ACT.Sigmoid,
                               bias=col("gate_b")[0:r, m:m + 1]).then_inc(s_sig, 1)

            def scores_of(j):
                a, n = PARTS[j]
                act.wait_ge(s_logits, j + 1)
                act.activation(scoresT[:, a:a + n], ps[0:EXPERTS, 7 if j == 0 else 4, 0:n], ACT.Sigmoid,
                               bias=col("router_b")[0:EXPERTS, :]).then_inc(s_scoresT, 1)

            def high_hid(w):
                m, j = UNITS[WEIGHED[w]]
                (a, n), r = PARTS[j], rows_of(m)
                act.wait_ge(s_hid, w + 1)
                if m >= BLOCK_SLOTS:
                    act.wait_ge(s_block_down, m - BLOCK_SLOTS + 1)
                act.activation(hid_hi[0:r, m % BLOCK_SLOTS, a:a + n], hid[0:r, w % H_SLOTS, 0:n],
                               ACT.Copy).then_inc(s_hid_hi, 1)

            def copy_up(u):
                m, j = UNITS[u]
                n, r, i = PARTS[j][1], rows_of(m), BY_POOL.index(u)
                act.wait_ge(s_up, u + 1)
                if i >= UP_SLOTS:
                    act.wait_ge(s_prod_pool, i - UP_SLOTS + 1)
                act.activation(up_b[0:r, i % UP_SLOTS, 0:n], ps[0:r, 2 + u % 2, 0:n], ACT.Identity,
                               bias=col("up_b")[0:r, m:m + 1]).then_inc(s_up_copied, 1)

            def split_down(i):
                a, n = (DOWN_CHUNKS + [MB])[i:i + 2]
                act.activation(down_hi[:, a:n, :], down_raw[:, a:n, :], ACT.Copy).then_inc(s_down_hi, 1)

            act.wait_ge(s_idle, 1)
            act.activation(sig_g[:, 0, 0:1], idle[:, 0:1], ACT.Sigmoid)
            high_of(0)
            act.wait_ge(s_xw, 16)
            for c, n in XW_SPLITS:
                act.activation(xw_hi[:, :, c:c + n], xw_raw[:, :, c:c + n], ACT.Copy).then_inc(s_xw_hi, 1)
            high_of(1)
            take_xT(0)
            high_of(2)
            take_xT(1)
            take_xT(2)
            high_of(3)
            high_of(4)
            copy_q(0)
            copy_kv(0)
            take_xT(3)
            copy_kv(1)
            take_xT(4)
            copy_kv(2)
            copy_q(1)
            act.wait_ge(s_small, 16)
            act.activation(w_proj_hi[:, :, :], w_proj[0:HALF_D, :, :], ACT.Copy).then_inc(s_w_proj_hi, 1)
            split_moe(0)
            copy_kv(3)
            split_moe(1)
            copy_kv(4)
            split_moe(2)
            split_moe(3)
            high_attn(0, 0)
            copy_kv(5)
            split_moe(4)
            high_attn(0, 1)
            copy_kv(6)
            split_moe(5)
            copy_kv(7)
            act.wait_ge(s_consts, 32)
            act.activation(down_b_hi[:, :], down_b_raw[:, :], ACT.Copy).then_inc(s_down_hi, 1)
            act.wait_ge(s_down_in, 16)
            split_down(0)
            split_down(1)
            act.activation(spread_sb[:, :], spread_raw, ACT.Copy).then_inc(s_spread, 1)
            high_attn(1, 0)
            high_of(5)
            high_attn(1, 1)
            high_of(6)
            take_xT(5)
            take_xT(6)
            high_of(7)
            sigmoid(0)
            sigmoid(1)
            take_xT(7)
            high_of(8)
            sigmoid(2)
            scores_of(0)
            high_of(9)
            take_xT(8)
            for step in range(STEPS):
                if step >= 1:
                    for w in WEIGH_AT[step - 1][1:]:
                        high_hid(w)
                if 3 <= step < NU:
                    sigmoid(step)
                    if step in BY_POOL:
                        copy_up(step)
                if step == ROUTE_AT - 1:
                    act.wait_ge(s_combine_ps, 1)
                    act.activation(combineT[:, 512:T], ps[0:CROWS, 6, 0:T - 512], ACT.Copy).then_inc(s_combineT, 1)
                if step == 3:
                    take_xT(9)
                if step == 4:
                    scores_of(1)
                for w in WEIGH_AT[step][:1]:
                    high_hid(w)
                if step in SPLIT_AT:
                    split_moe(SPLIT_AT[step])
                if step in DOWN_SPLIT_AT:
                    split_down(DOWN_SPLIT_AT[step])
            for w in WEIGH_AT[STEPS - 1][1:]:
                high_hid(w)

        @block.gpsimd
        def _(pool):
            links = [0]

            def link(ins):
                links[0] += 1
                ins.then_inc(s_pool, 1)
                pool.wait_ge(s_pool, links[0])

            def low(o, x, hi, done):
                pool.tensor_tensor(o, x, hi.bitcast(f32), ALU.subtract).then_inc(done, 1)

            def split_moe(m):
                c = m // CHUNK
                w = 4 * rows_of(m)
                pool.wait_ge(s_moe_hi, m + 1)
                low(moe_lo[:, m % MOE_SLOTS, 0:w], moe_raw[:, c % RAW_SLOTS, 512 * (m % CHUNK):512 * (m % CHUNK) + w],
                    moe_hi[:, m % MOE_SLOTS, 0:w], s_moe_lo)

            def root_of(t):
                n = TILES[t % NT][1]
                pool.wait_ge(s_var, t + 1)
                pool.tensor_tensor(root[0:n, t, 1:2], root[0:n, t, 0:1], half_power[0:n, :], ALU.pow).then_inc(s_root, 1)

            def low_tok(t):
                n = TILES[t % NT][1]
                pool.wait_ge(s_tok_hi, t + 1)
                pool.tensor_tensor(split_tok[0:n, t % 3, D:D + 64], normed[0:n, t % 3, 128:D],
                                   split_f[0:n, t % 3, 128:D], ALU.subtract)
                pool.tensor_tensor(split_tok[0:n, t % 3, D + 64:2 * D], normed[0:n, t % 3, 0:128],
                                   split_f[0:n, t % 3, 0:128], ALU.subtract).then_inc(s_tok_lo, 1)

            def low_down(i):
                a, n = (DOWN_CHUNKS + [MB])[i:i + 2]
                pool.wait_ge(s_down_hi, i + 2)
                low(down_lo[:, a:n, :], down_raw[:, a:n, :], down_hi[:, a:n, :], s_down_lo)

            def mask_groups():
                pool.wait_ge(s_beaten, 2)
                for i, order in enumerate(("before", "after")):
                    ins = pool.tensor_tensor(beaten[:, i, :, :], beaten[:, i, :, :],
                                             col(order).unsqueeze(1).broadcast_to([128, NT, GROUPS * GROUPS]), ALU.mult)
                link(ins)
                link(pool.tensor_tensor(beaten[:, 0, :, :], beaten[:, 0, :, :], beaten[:, 1, :, :], ALU.add))
                by = beaten[:, 0, :, :].rearrange("p t (g o) -> p (t g) o", o=GROUPS)
                link(pool.tensor_tensor(by[:, :, 0:2], by[:, :, 0:2], by[:, :, 2:4], ALU.add))
                link(pool.tensor_tensor(rank[:, :, :].rearrange("p t g -> p (t g)").unsqueeze(2),
                                        by[:, :, 0:1], by[:, :, 1:2], ALU.add))
                link(pool.tensor_scalar(rank[:, :, :], rank[:, :, :], TOP_GROUPS - 0.5, None, ALU.is_lt))
                g = rank[:, :, :].unsqueeze(3).broadcast_to([128, NT, GROUPS, PER_GROUP])
                link(pool.tensor_tensor(choice[:, :, :].rearrange("p t (g e) -> p t g e", e=PER_GROUP),
                                        choice[:, :, :].rearrange("p t (g e) -> p t g e", e=PER_GROUP), g, ALU.mult))
                pool.tensor_scalar(masked[:, :, 0:EXPERTS], choice[:, :, :], 0.0, None, ALU.add).then_inc(s_masked, 1)

            def scale_q(j):
                for m in range(2):
                    q = qT[:, m, HALF_T * j:HALF_T * (j + 1)].rearrange("p (i t) -> p i t", t=TOK)
                    pool.wait_ge(s_q_copied, 2 * j + m + 1)
                    pool.wait_ge(s_scale, j + 1)
                    pool.tensor_tensor(q, q, scale_qk[:, j, m, :].unsqueeze(2).broadcast_to([HALF_D, HALF_I, TOK]),
                                       ALU.mult).then_inc(s_qT, 1)

            pool.memset(x1T[:, :, :, TOK:SLOT].bitcast(f32), 0.0)
            pool.memset(half_power[:, :], -0.5)
            pool.memset(scores[:, :, :], 0.0)
            pool.memset(masked[:, :, :], PAD)
            pool.memset(taken8[:, :, :], PAD)
            pool.memset(combine_split[:, :, 2 * EXPERTS:CROWS].bitcast(f32), 1.0).then_inc(s_zero, 1)
            def low_xw(c, n, i):
                low(xw_lo[:, i, c:c + n], xw_raw[:, i, c:c + n], xw_hi[:, i, c:c + n], s_xw_lo)

            pool.wait_ge(s_zero, 1)
            root_of(0)
            root_of(1)
            low_tok(0)
            root_of(2)
            pool.wait_ge(s_xw_hi, 1)
            low_xw(*XW_SPLITS[0], 0)
            low_tok(1)
            root_of(3)
            low_tok(2)
            root_of(4)
            pool.wait_ge(s_xw_hi, 2)
            low_xw(*XW_SPLITS[1], 0)
            low_tok(3)
            low_xw(*XW_SPLITS[1], 1)
            low_tok(4)
            scale_q(0)
            pool.wait_ge(s_small, 16)
            for t, (a, n) in enumerate(TILES):
                pool.wait_ge(s_h, t + 1)
                pool.tensor_tensor(h2_tok[0:n, t, :], h_tok[0:n, t, :], col("b_proj")[0:n, :], ALU.add).then_inc(s_hb, 1)
            scale_q(1)
            pool.wait_ge(s_w_proj_hi, 1)
            low(w_proj_lo[:, :, :], w_proj[0:HALF_D, :, :], w_proj_hi[:, :, :], s_w_proj_lo)
            for m in range(FIRST_SPLITS):
                split_moe(m)
            pool.wait_ge(s_down_hi, 1)
            low(down_b_lo[:, :], down_b_raw[:, :], down_b_hi[:, :], s_down_lo)
            low_down(0)
            root_of(5)
            root_of(6)
            low_tok(5)
            low_tok(6)
            low_down(1)
            root_of(7)
            root_of(8)
            low_tok(7)
            root_of(9)
            low_tok(8)
            low_tok(9)
            for step in range(STEPS):
                if step == SCORES_AT:
                    mask_groups()
                if step in BY_POOL:
                    i = BY_POOL.index(step)
                    m, j = UNITS[step]
                    n, r = PARTS[j][1], rows_of(m)
                    p = prod[0:r, step % T_SLOTS, 0:n]
                    pool.wait_ge(s_gated, step + 1)
                    pool.wait_ge(s_up_copied, i + 1)
                    pool.tensor_tensor(p, p, up_b[0:r, i % UP_SLOTS, 0:n], ALU.mult).then_inc(s_prod_pool, 1)
                for w in WEIGH_AT[step]:
                    m, j = UNITS[WEIGHED[w]]
                    (a, n), r = PARTS[j], rows_of(m)
                    pool.wait_ge(s_hid_hi, w + 1)
                    low(hid_lo[0:r, m % BLOCK_SLOTS, a:a + n], hid[0:r, w % H_SLOTS, 0:n],
                        hid_hi[0:r, m % BLOCK_SLOTS, a:a + n], s_hid_lo)
                if step in SPLIT_AT:
                    split_moe(SPLIT_AT[step])
                if step in DOWN_SPLIT_AT:
                    low_down(DOWN_SPLIT_AT[step])

        @block.vector
        def _(dve):
            links = [0]

            def mark(ins):
                links[0] += 1
                ins.then_inc(s_dve, 1)
                return links[0]

            def link(ins):
                dve.wait_ge(s_dve, mark(ins))

            def layer_norm(tiles, first, h, between=None):
                for i in range(len(tiles) + 1):
                    new = first + tiles[i] if i < len(tiles) else None
                    old = first + tiles[i - 1] if 1 <= i <= len(tiles) else None
                    if new is not None:
                        t, n = new, TILES[new % NT][1]
                        row, s_row = h(t % NT)
                    if old is not None:
                        o, k = old, TILES[old % NT][1]
                        v, g, y = (root[0:k, o, c:c + 1] for c in (0, 1, 2))
                    if new is not None:
                        dve.wait_ge(*s_row)
                        a = mark(dve.bn_stats(stats[0:n, t % 2, :], row))
                    if old is not None:
                        dve.wait_ge(s_root, o + 1)
                        y_at = mark(dve.scalar_tensor_tensor(out=y, in0=g, scalar=v, in1=g, op0=ALU.mult, op1=ALU.mult))
                    if new is not None:
                        dve.wait_ge(s_dve, a)
                        a = mark(dve.bn_aggr(mean_var[0:n, t, :], stats[0:n, t % 2, :]))
                    if old is not None:
                        dve.wait_ge(s_dve, y_at)
                        c_at = mark(dve.tensor_scalar(root[0:k, o, 3:4], y, -0.5, 1.5, ALU.mult, ALU.add))
                    if new is not None:
                        dve.wait_ge(s_dve, a)
                        dve.tensor_scalar(root[0:n, t, 0:1], mean_var[0:n, t, 1:2], LN_EPS, None, ALU.add).then_inc(s_var, 1)
                    if old is not None:
                        dve.wait_ge(s_dve, c_at)
                        y_at = mark(dve.tensor_tensor(root[0:k, o, 4:5], root[0:k, o, 3:4], g, ALU.mult))
                    if old is not None:
                        if o >= 3:
                            dve.wait_ge(s_tok_lo, o - 2)
                        dve.wait_ge(s_dve, y_at)
                        hrow = (h_tok if first == 0 else h2_tok)[0:k, o % NT, :]
                        dve.tensor_scalar(normed[0:k, o % 3, :], hrow, mean_var[0:k, o, 0:1], root[0:k, o, 4:5],
                                          ALU.subtract, ALU.mult).then_inc(s_normed, 1)
                    if between:
                        between(i)

            def base_of(t):
                n = TILES[t][1]
                dve.wait_ge(s_first if t < 2 else s_second, 16)
                dve.scalar_tensor_tensor(out=base[0:n, t, :], in0=col("b")[0:n, :],
                                         scalar=col("token_is_patch")[0:n, t:t + 1], in1=base[0:n, t, :],
                                         op0=ALU.mult, op1=ALU.add).then_inc(s_base, 1)

            def base_between(i):
                if i + 2 < NT:
                    base_of(i + 2)
                if i == NT - 2:
                    c, n = XW_SPLITS[0]
                    dve.wait_ge(s_xw_hi, 1)
                    dve.tensor_tensor(xw_lo[:, 1, c:c + n], xw_raw[:, 1, c:c + n], xw_hi[:, 1, c:c + n].bitcast(f32),
                                      ALU.subtract).then_inc(s_xw_lo_1, 1)

            def embedded(t):
                n = TILES[t][1]
                dve.wait_ge(s_embed, t + 1)
                dve.wait_ge(s_base, t + 1)
                dve.tensor_tensor(h_tok[0:n, t, :], ps[0:n, t % 2, 0:D], base[0:n, t, :], ALU.add).then_inc(s_h, 1)
                return h_tok[0:n, t, :], (s_h, t + 1)

            def attended(t):
                n = TILES[t][1]
                dve.wait_ge(s_proj, t + 1)
                dve.wait_ge(s_hb, t + 1)
                dve.tensor_tensor(h2_tok[0:n, t, :], ps[0:n, proj_bank[t], 0:D], h2_tok[0:n, t, :],
                                  ALU.add).then_inc(s_h2, 1)
                return h2_tok[0:n, t, :], (s_h2, t + 1)

            def qk_sums(j):
                for kind, ready, bank in ((0, s_k, 4), (1, s_q, 6)):
                    for m in range(2):
                        dve.wait_ge(ready, 2 * j + m + 1)
                        dve.tensor_reduce(sums[:, j, kind, m, :],
                                          ps[0:HALF_D, bank + m, 0:HALF_I * EVEN]
                                          .rearrange("p (i t) -> p i t", t=EVEN)[:, :, 0:TOK],
                                          AX.X, ALU.add, apply_absolute_value=True).then_inc(s_qk_summed, 1)

            def qk_scale(j):
                dve.wait_ge(s_qk_summed, 4 * (j + 1))
                link(dve.tensor_scalar(sums[:, j, :, :, :], sums[:, j, :, :, :], L1_EPS, None, ALU.max))
                link(dve.reciprocal(sums[:, j, :, :, :], sums[:, j, :, :, :]))
                dve.tensor_tensor(scale_qk[:, j, :, :], sums[:, j, 0, :, :], sums[:, j, 1, :, :],
                                  ALU.mult).then_inc(s_scale, 1)

            def mask(p):
                dve.wait_ge(s_outer, p + 1)
                b = 2 + 2 * (p % 2)
                dve.tensor_tensor(kv_blocks[:, 2 * p:2 * p + 2, :], ps[0:HALF_D, b:b + 2, 0:D],
                                  col("blocks")[0:HALF_D, :].unsqueeze(1).broadcast_to([HALF_D, 2, D]),
                                  ALU.mult).then_inc(s_blocks, 1)

            def low_attn(j, m):
                tok = slice(HALF_T * j, HALF_T * (j + 1))
                dve.wait_ge(s_attn_hi, 2 * j + m + 1)
                dve.tensor_tensor(attn_lo[:, m, tok], ps[0:HALF_D, 6 + m, 0:HALF_T],
                                  attn_hi[:, m, tok].bitcast(f32), ALU.subtract).then_inc(s_attn_lo, 1)

            dve.memset(idle[:, :], 0.0).then_inc(s_idle, 1)
            base_of(0)
            base_of(1)
            layer_norm(range(NT), 0, embedded, base_between)
            qk_sums(0)
            qk_scale(0)
            dve.wait_ge(s_small, 16)
            mask(0)
            qk_sums(1)
            mask(1)
            qk_scale(1)
            mask(2)
            mask(3)
            low_attn(0, 0)
            mask(4)
            low_attn(0, 1)
            mask(5)

            def low_between(i):
                if i == 0:
                    mask(6)
                    mask(7)
                if i == 1:
                    low_attn(1, 0)

            layer_norm((0, 1), NT, attended, low_between)
            low_attn(1, 1)
            def gated(u):
                m, j = UNITS[u]
                n, r = PARTS[j][1], rows_of(m)
                dve.wait_ge(s_gate, u + 1)
                dve.wait_ge(s_sig, u + 1)
                dve.scalar_tensor_tensor(out=prod[0:r, u % T_SLOTS, 0:n], in0=ps[0:r, u % 2, 0:n],
                                         scalar=col("gate_b")[0:r, m:m + 1], in1=sig_g[0:r, u % S_SLOTS, 0:n],
                                         op0=ALU.add, op1=ALU.mult).then_inc(s_gated, 1)

            def times_up(u):
                m, j = UNITS[u]
                n, r = PARTS[j][1], rows_of(m)
                dve.wait_ge(s_up, u + 1)
                dve.wait_ge(s_gated, u + 1)
                dve.scalar_tensor_tensor(out=prod[0:r, u % T_SLOTS, 0:n], in0=ps[0:r, 2 + u % 2, 0:n],
                                         scalar=col("up_b")[0:r, m:m + 1], in1=prod[0:r, u % T_SLOTS, 0:n],
                                         op0=ALU.add, op1=ALU.mult).then_inc(s_prod, 1)

            def weigh(w):
                u = WEIGHED[w]
                m, j = UNITS[u]
                n, r = PARTS[j][1], rows_of(m)
                if u in BY_POOL:
                    dve.wait_ge(s_prod_pool, BY_POOL.index(u) + 1)
                else:
                    dve.wait_ge(s_prod, by_vector(u))
                if w >= H_SLOTS:
                    dve.wait_ge(s_hid_lo, w - H_SLOTS + 1)
                if m >= SHARED_MB:
                    dve.wait_ge(s_spread_ps, w - N_SHARED_UNITS + 1)
                    dve.tensor_tensor(hid[0:r, w % H_SLOTS, 0:n], prod[0:r, u % T_SLOTS, 0:n],
                                      ps[0:r, 7, 0:n], ALU.mult).then_inc(s_hid, 1)
                else:
                    dve.tensor_copy(hid[0:r, w % H_SLOTS, 0:n], prod[0:r, u % T_SLOTS, 0:n]).then_inc(s_hid, 1)

            def take_scores():
                dve.wait_ge(s_zero, 1)
                dve.wait_ge(s_scores_ps, 1)
                full = NT - 1
                n = TILES[full][1]
                dve.tensor_copy(scores[:, 0:full, :],
                                ps[:, 5, 0:EXPERTS * full].rearrange("p (t e) -> p t e", e=EXPERTS)).then_inc(s_scores, 1)
                dve.tensor_copy(scores[0:n, full, :], ps[0:n, 5, EXPERTS * full:EXPERTS * NT]).then_inc(s_scores, 1)
                dve.wait_ge(s_scores, 2)
                link(dve.tensor_tensor(choice[:, :, :], scores[:, :, :],
                                       col("corr").unsqueeze(1).broadcast_to([128, NT, EXPERTS]), ALU.add))

            def group_scores():
                c = choice[:, :, :].rearrange("p t (g e) -> p (t g) e", e=PER_GROUP)
                dve.tensor_tensor(pair_sums[:, :, 0:2], c[:, :, 0:2], c[:, :, 2:4], ALU.add)
                dve.tensor_tensor(pair_sums[:, :, 2:4], c[:, :, 0:4:2], c[:, :, 1:4:2], ALU.add)
                dve.tensor_tensor(pair_sums[:, :, 4:5], c[:, :, 0:1], c[:, :, 3:4], ALU.add)
                link(dve.tensor_tensor(pair_sums[:, :, 5:6], c[:, :, 1:2], c[:, :, 2:3], ALU.add))
                link(dve.tensor_reduce(group_s[:, :, :], pair_sums[:, :, :], AX.X, ALU.max))

            def compare_groups():
                for i, op in enumerate((ALU.is_ge, ALU.is_gt)):
                    out4 = beaten[:, i, :, :].rearrange("p t (g o) -> p t g o", o=GROUPS)
                    dve.tensor_tensor(out4, group_s[:, :, :].unsqueeze(2).broadcast_to([128, NT, GROUPS, GROUPS]),
                                      group_s[:, :, :].unsqueeze(3).broadcast_to([128, NT, GROUPS, GROUPS]),
                                      op).then_inc(s_beaten, 1)

            def expert_choice():
                dve.wait_ge(s_masked, 1)
                for t in range(NT):
                    ins = dve.max(top8[:, t, :], masked[:, t, 0:EXPERTS])
                link(ins)
                link(dve.tensor_copy(taken8[:, :, 0:TOP_K], top8[:, :, 0:TOP_K]))
                for t in range(NT):
                    ins = dve.match_replace(marked[:, t, :], taken8[:, t, :], masked[:, t, :], TAKEN)
                link(ins)

            def chosen_sums():
                link(dve.scalar_tensor_tensor(out=weight[:, :, :], in0=marked[:, :, 0:EXPERTS], scalar=TAKEN,
                                              in1=scores[:, :, :], op0=ALU.is_equal, op1=ALU.mult))
                link(dve.tensor_reduce(w_sum[:, 0, :], weight[:, :, :], AX.X, ALU.add))
                link(dve.tensor_scalar(w_sum[:, 1, :], w_sum[:, 0, :], SUM_EPS, None, ALU.add))
                link(dve.reciprocal(w_sum[:, 2, :], w_sum[:, 1, :]))

            def combine_weights():
                link(dve.scalar_tensor_tensor(out=combine[:, :, :], in0=weight[:, :, :], scalar=SCALE,
                                              in1=w_sum[:, 2, :].unsqueeze(2).broadcast_to([128, NT, EXPERTS]),
                                              op0=ALU.mult, op1=ALU.mult))
                link(dve.tensor_copy(combine_split[:, :, 0:EXPERTS], combine[:, :, :]))
                dve.tensor_tensor(combine_split[:, :, EXPERTS:2 * EXPERTS], combine[:, :, :],
                                  combine_split_f[:, :, 0:EXPERTS], ALU.subtract).then_inc(s_combine, 1)

            def take_combine():
                dve.wait_ge(s_combine_ps, 1)
                dve.tensor_copy(combineT[:, 0:512], ps[0:CROWS, 7, 0:512]).then_inc(s_combineT, 1)

            def gated_between(i):
                if i == 1:
                    gated(0)
                if i == 2:
                    times_up(0)
                    gated(1)

            layer_norm((2, 3, 4), NT, attended, gated_between)
            for step in range(STEPS):
                if step == SCORES_AT:
                    take_scores()
                    group_scores()
                    compare_groups()
                if step == ROUTE_AT:
                    take_combine()
                weigh_now = WEIGH_AT[step]
                for w in weigh_now[:1]:
                    weigh(w)
                if 2 <= step < NU:
                    gated(step)
                if step == CHOOSE_AT:
                    expert_choice()
                if step == SUMS_AT:
                    chosen_sums()
                if step == WEIGHTS_AT:
                    combine_weights()
                if 1 <= step < NU and step not in BY_POOL:
                    times_up(step)
                for w in weigh_now[1:]:
                    weigh(w)

            for bank in range(4, 4 + (NT + 1) // 2):
                t = 2 * (bank - 4)
                tiles, n = min(2, NT - t), TILES[t][1]
                dve.wait_ge(s_down, t + tiles)
                dve.tensor_tensor(h2_tok[0:n, t:t + tiles, :],
                                  ps[0:n, bank, 0:D * tiles].rearrange("p (t d) -> p t d", d=D),
                                  h2_tok[0:n, t:t + tiles, :], ALU.add).then_inc(s_out_tok, 1)


def kernel(**inputs):
    import concourse.bacc as _bacc
    from concourse.bass_utils import run_bass_kernel_spmd as _run

    g = {k.replace("L0_", ""): np.asarray(v) for k, v in inputs.items()}
    f = np.float32

    def rows128(a):
        k = -(-a.shape[0] // 128)
        full = np.zeros((k * 128, a.shape[1]), f)
        full[:a.shape[0]] = a
        return full.reshape(k, 128, -1).transpose(1, 0, 2)

    def blocks128(shared, routed):
        return np.concatenate([rows128(shared), rows128(routed)], axis=1)

    x = g["x"].reshape(IMAGES, CHANNELS, GRID, PATCH, GRID, PATCH).transpose(1, 3, 5, 0, 2, 4)
    cols = np.zeros((CHANNELS * PATCH * PATCH, IMAGES, TOK), f)
    cols[:, :, 1:] = x.reshape(-1, IMAGES, GRID * GRID)
    cols = rows128(cols.reshape(-1, T))
    patches = np.concatenate([cols[:, :, a:a + n].reshape(128, -1) for a, n in TILES], axis=1)

    near = np.arange(GRID) * POS_SIDE // GRID
    pos = g["tok_positions"][0][:, near][:, :, near].reshape(D, -1).T
    base = np.concatenate([g["tok_cls_embedding"].reshape(1, D), pos])
    small = np.zeros((128, SMALL_COLS), f)

    def put(name, a, rows=128):
        lo, hi = COLS[name]
        small[:rows, lo:hi] = a

    put("ident", np.eye(128, dtype=f))
    put("token_is_patch", rows128((np.arange(T) % TOK > 0).astype(f)[:, None])[:, :, 0])
    put("b", g["tok_b"][None])
    put("base", rows128(np.tile(base, (IMAGES, 1))).reshape(128, -1))
    patch_w = rows128(g["tok_W"]).reshape(128, -1)
    heads = np.arange(HALF_D) // HEAD
    put("blocks", np.tile((heads[:, None] == heads).astype(f), (1, 2)), HALF_D)
    put("b_proj", g["attn_b_proj"][None])
    put("w_proj", g["attn_w_proj"].T.reshape(2, HALF_D, D).transpose(1, 0, 2).reshape(HALF_D, -1), HALF_D)
    put("router_b", g["ffn_router_b"][:, None], EXPERTS)
    put("corr", g["ffn_corr_bias"][None])
    k = np.arange(GROUPS)
    put("before", (k < k[:, None]).astype(f).reshape(1, -1))
    put("after", (k > k[:, None]).astype(f).reshape(1, -1))
    for name, routed, shared in (("gate_b", "gbg", "sbg"), ("up_b", "gbu", "sbu")):
        put(name, blocks128(g[f"ffn_{shared}"][:, None], g[f"ffn_{routed}"].reshape(-1, 1))[:, :, 0])

    def x_side(w):
        return np.stack([w[:128], np.concatenate([w[128:], w[128:]])], axis=1)

    x_w = x_side(np.concatenate([g["attn_w_qkv"].T, g["ffn_router_w"].T], axis=1))
    gate, up = (x_side(np.concatenate([g[f"ffn_{s}"], g[f"ffn_{r}"].transpose(1, 0, 2).reshape(D, ROUTED)], axis=1))
                for r, s in (("gWg", "sWg"), ("gWu", "sWu")))
    moe_w = np.zeros((128, MB, 512), f)
    for m, (a, n) in enumerate(BLOCKS):
        moe_w[:, m, :4 * n] = np.concatenate([w[:, :, a:a + n].reshape(128, -1) for w in (gate, up)], axis=1)
    moe_w = moe_w.reshape(128, -1)
    down_w = blocks128(g["ffn_sWd"], g["ffn_gWd"].reshape(ROUTED, D))
    down_b = np.concatenate([g["ffn_gbd"], g["ffn_gbd"], g["ffn_sbd"][None]])
    of = (np.arange(ROUTED) // INNER == np.arange(EXPERTS)[:, None]).astype(f)
    spread = np.concatenate([of, of, np.zeros((1, ROUTED), f)])

    nc = _bacc.Bacc("TRN2", target_bir_lowering=False, num_devices=1)
    arrays, args = {}, []
    for name, a in (("patches", patches), ("patch_w", patch_w), ("small", small), ("x_w", x_w), ("moe_w", moe_w),
                    ("down_w", down_w), ("down_b", down_b), ("spread", spread)):
        a = np.ascontiguousarray(a)
        arrays[f"in_{name}"] = a
        args.append(nc.dram_tensor(f"in_{name}", a.shape, mybir.dt.from_np(a.dtype), kind="ExternalInput").ap())
    args.append(nc.dram_tensor("out_tokens", (T, D), mybir.dt.float32, kind="ExternalOutput").ap())
    tower(nc, *args)
    r = _run(nc, [arrays], core_ids=[0])
    return r.results[0]["out_tokens"].reshape(IMAGES, TOK, D)
```
